# Optimizing a Trainium2 kernel written in Bass

```python
import numpy as np
import jax
import jax.numpy as jnp

def _softmax(x, axis=-1):
    return jax.nn.softmax(x, axis=axis)

def _gelu(x):
    return jax.nn.gelu(x, approximate=True)

def _silu(x):
    return jax.nn.silu(x)

def _sigmoid(x):
    return jax.nn.sigmoid(x)

def _layernorm(x, axis=-1, eps=1e-05):
    m = jnp.mean(x, axis=axis, keepdims=True)
    v = jnp.var(x, axis=axis, keepdims=True)
    return (x - m) / jnp.sqrt(v + eps)

def _scatter_add(tgt, idx, src, axis=0):
    return tgt.at[idx].add(src)

def _segment_sum(src, seg, n):
    return jax.ops.segment_sum(src, seg, n)
kernel_name = 'mk_adaln_d1_jaxref_r8_2e1930'

def setup_inputs(seed: int=0):
    np.random.seed(seed)
    _w = jnp.asarray

    def _L0_attn_setup():
        import jax, jax.numpy as jnp
        import numpy as np
        B, L, H, I, K, G = (2, 512, 128, 256, 4, 8)
        EPS = 1e-05

        def _layernorm(x, g, b):
            m = x.mean(-1, keepdims=True)
            v = jnp.var(x, axis=-1, keepdims=True)
            return (x - m) * jax.lax.rsqrt(v + EPS) * g + b
        key = jax.random.key(seed)
        ks = jax.random.split(key, 8)
        s = 0.02
        return {'hidden_states': jax.random.normal(ks[0], (B, L, H), jnp.float32), 'in_proj_w': jax.random.normal(ks[1], (2 * I, H), jnp.float32) * s, 'conv_w': jax.random.normal(ks[2], (I, I // G, K), jnp.float32) * s, 'conv_b': jax.random.normal(ks[3], (I,), jnp.float32) * s, 'ln_g': jnp.ones((I,), jnp.float32), 'ln_b': jnp.zeros((I,), jnp.float32), 'fc_w': jax.random.normal(ks[4], (H, I), jnp.float32) * s, 'fc_b': jnp.zeros((H,), jnp.float32), 'cproj_w': jax.random.normal(ks[5], (I, H), jnp.float32) * s, 'cproj_b': jnp.zeros((I,), jnp.float32), 'out_w': jax.random.normal(ks[6], (H, I), jnp.float32) * s}
    _L0_attn_in = _L0_attn_setup()

    def _L0_ffn_setup():
        import jax, jax.numpy as jnp
        import numpy as np
        B, L, D = (4, 256, 128)
        H = 16
        E = 16
        NS = 16
        S = NS // E
        F = 512
        EPS = 1e-05

        def _layernorm(x, g, b):
            mu = jnp.mean(x, axis=-1, keepdims=True)
            var = jnp.mean(jnp.square(x - mu), axis=-1, keepdims=True)
            return (x - mu) * jax.lax.rsqrt(var + EPS) * g + b

        def _mha(q, k, v, Wq, bq, Wk, bk, Wv, bv, Wo, bo):
            Bq, Lq, Dm = q.shape
            dh = Dm // H
            qh = (q @ Wq + bq).reshape(Bq, Lq, H, dh)
            kh = (k @ Wk + bk).reshape(Bq, -1, H, dh)
            vh = (v @ Wv + bv).reshape(Bq, -1, H, dh)
            scores = jnp.einsum('bqhd,bkhd->bhqk', qh, kh) / jnp.asarray(np.sqrt(dh), q.dtype)
            attn = jax.nn.softmax(scores, axis=-1)
            out = jnp.einsum('bhqk,bkhd->bqhd', attn, vh).reshape(Bq, Lq, Dm)
            return out @ Wo + bo
        key = jax.random.key(seed)
        ks = jax.random.split(key, 32)
        s = 0.02
        d = {}
        d['x'] = jax.random.normal(ks[0], (B, L, D), jnp.float32)
        d['slot_query'] = jax.random.normal(ks[1], (1, NS, D), jnp.float32) * 0.01
        for i, nm in enumerate(['d_Wq', 'd_Wk', 'd_Wv', 'd_Wo']):
            d[nm] = jax.random.normal(ks[2 + i], (D, D), jnp.float32) * s
        for nm in ['d_bq', 'd_bk', 'd_bv', 'd_bo']:
            d[nm] = jnp.zeros((D,), jnp.float32)
        for i, nm in enumerate(['c_Wq', 'c_Wk', 'c_Wv', 'c_Wo']):
            d[nm] = jax.random.normal(ks[6 + i], (D, D), jnp.float32) * s
        for nm in ['c_bq', 'c_bk', 'c_bv', 'c_bo']:
            d[nm] = jnp.zeros((D,), jnp.float32)
        d['e_ln_g'] = jnp.ones((E, D), jnp.float32)
        d['e_ln_b'] = jnp.zeros((E, D), jnp.float32)
        d['e_W1'] = jax.random.normal(ks[10], (E, D, F), jnp.float32) * s
        d['e_b1'] = jnp.zeros((E, F), jnp.float32)
        d['e_Wg'] = jax.random.normal(ks[11], (E, D, F), jnp.float32) * s
        d['e_bg'] = jnp.zeros((E, F), jnp.float32)
        d['e_W2'] = jax.random.normal(ks[12], (E, F, D), jnp.float32) * s
        d['e_b2'] = jnp.zeros((E, D), jnp.float32)
        return d
    _L0_ffn_in = _L0_ffn_setup()
    _L0_c = _w((lambda *s: np.random.randn(*s).astype(np.float32) * 0.05)(16, 128))
    _L0_wmod = _w((lambda *s: np.random.randn(*s).astype(np.float32) * 0.05)(128, 6 * 128) * 128 ** (-0.5))
    _d = {'L0_attn_hidden_states': _L0_attn_in['hidden_states'], 'L0_attn_in_proj_w': _L0_attn_in['in_proj_w'], 'L0_attn_conv_w': _L0_attn_in['conv_w'], 'L0_attn_conv_b': _L0_attn_in['conv_b'], 'L0_attn_ln_g': _L0_attn_in['ln_g'], 'L0_attn_ln_b': _L0_attn_in['ln_b'], 'L0_attn_fc_w': _L0_attn_in['fc_w'], 'L0_attn_fc_b': _L0_attn_in['fc_b'], 'L0_attn_cproj_w': _L0_attn_in['cproj_w'], 'L0_attn_cproj_b': _L0_attn_in['cproj_b'], 'L0_attn_out_w': _L0_attn_in['out_w'], 'L0_ffn_slot_query': _L0_ffn_in['slot_query'], 'L0_ffn_d_Wq': _L0_ffn_in['d_Wq'], 'L0_ffn_d_Wk': _L0_ffn_in['d_Wk'], 'L0_ffn_d_Wv': _L0_ffn_in['d_Wv'], 'L0_ffn_d_Wo': _L0_ffn_in['d_Wo'], 'L0_ffn_d_bq': _L0_ffn_in['d_bq'], 'L0_ffn_d_bk': _L0_ffn_in['d_bk'], 'L0_ffn_d_bv': _L0_ffn_in['d_bv'], 'L0_ffn_d_bo': _L0_ffn_in['d_bo'], 'L0_ffn_c_Wq': _L0_ffn_in['c_Wq'], 'L0_ffn_c_Wk': _L0_ffn_in['c_Wk'], 'L0_ffn_c_Wv': _L0_ffn_in['c_Wv'], 'L0_ffn_c_Wo': _L0_ffn_in['c_Wo'], 'L0_ffn_c_bq': _L0_ffn_in['c_bq'], 'L0_ffn_c_bk': _L0_ffn_in['c_bk'], 'L0_ffn_c_bv': _L0_ffn_in['c_bv'], 'L0_ffn_c_bo': _L0_ffn_in['c_bo'], 'L0_ffn_e_ln_g': _L0_ffn_in['e_ln_g'], 'L0_ffn_e_ln_b': _L0_ffn_in['e_ln_b'], 'L0_ffn_e_W1': _L0_ffn_in['e_W1'], 'L0_ffn_e_b1': _L0_ffn_in['e_b1'], 'L0_ffn_e_Wg': _L0_ffn_in['e_Wg'], 'L0_ffn_e_bg': _L0_ffn_in['e_bg'], 'L0_ffn_e_W2': _L0_ffn_in['e_W2'], 'L0_ffn_e_b2': _L0_ffn_in['e_b2'], 'L0_c': _L0_c, 'L0_wmod': _L0_wmod}
    _x0 = _d['L0_attn_hidden_states']
    _d['L0_attn_hidden_states'] = jax.random.normal(jax.random.fold_in(jax.random.key(seed), 1), (16, 256, 128), dtype=_x0.dtype)
    del _x0
    return _d

def reference(L0_attn_hidden_states, L0_attn_in_proj_w, L0_attn_conv_w, L0_attn_conv_b, L0_attn_ln_g, L0_attn_ln_b, L0_attn_fc_w, L0_attn_fc_b, L0_attn_cproj_w, L0_attn_cproj_b, L0_attn_out_w, L0_ffn_slot_query, L0_ffn_d_Wq, L0_ffn_d_Wk, L0_ffn_d_Wv, L0_ffn_d_Wo, L0_ffn_d_bq, L0_ffn_d_bk, L0_ffn_d_bv, L0_ffn_d_bo, L0_ffn_c_Wq, L0_ffn_c_Wk, L0_ffn_c_Wv, L0_ffn_c_Wo, L0_ffn_c_bq, L0_ffn_c_bk, L0_ffn_c_bv, L0_ffn_c_bo, L0_ffn_e_ln_g, L0_ffn_e_ln_b, L0_ffn_e_W1, L0_ffn_e_b1, L0_ffn_e_Wg, L0_ffn_e_bg, L0_ffn_e_W2, L0_ffn_e_b2, L0_c, L0_wmod):

    def _L0_attn_ref(hidden_states, in_proj_w, conv_w, conv_b, ln_g, ln_b, fc_w, fc_b, cproj_w, cproj_b, out_w):
        import jax, jax.numpy as jnp
        import numpy as np
        B, L, H, I, K, G = (2, 512, 128, 256, 4, 8)
        EPS = 1e-05

        def _layernorm(x, g, b):
            m = x.mean(-1, keepdims=True)
            v = jnp.var(x, axis=-1, keepdims=True)
            return (x - m) * jax.lax.rsqrt(v + EPS) * g + b
        p = hidden_states @ in_proj_w.T
        h, gate = (p[..., :I], p[..., I:])
        gate = jax.nn.silu(gate)
        hc = jnp.transpose(h, (0, 2, 1))
        conv = jax.lax.conv_general_dilated(hc, conv_w, window_strides=(1,), padding=[(K - 1, 0)], feature_group_count=G, dimension_numbers=('NCH', 'OIH', 'NCH'))
        conv = conv + conv_b[None, :, None]
        h = jnp.transpose(conv, (0, 2, 1)) * gate
        residual = h
        hn = _layernorm(h, ln_g, ln_b)
        m = jax.nn.silu(hn @ fc_w.T + fc_b) @ cproj_w.T + cproj_b
        h = m + residual
        return h @ out_w.T

    def _L0_ffn_ref(x, slot_query, d_Wq, d_Wk, d_Wv, d_Wo, d_bq, d_bk, d_bv, d_bo, c_Wq, c_Wk, c_Wv, c_Wo, c_bq, c_bk, c_bv, c_bo, e_ln_g, e_ln_b, e_W1, e_b1, e_Wg, e_bg, e_W2, e_b2):
        import jax, jax.numpy as jnp
        import numpy as np
        B, L, D = (4, 256, 128)
        H = 16
        E = 16
        NS = 16
        S = NS // E
        F = 512
        EPS = 1e-05

        def _layernorm(x, g, b):
            mu = jnp.mean(x, axis=-1, keepdims=True)
            var = jnp.mean(jnp.square(x - mu), axis=-1, keepdims=True)
            return (x - mu) * jax.lax.rsqrt(var + EPS) * g + b

        def _mha(q, k, v, Wq, bq, Wk, bk, Wv, bv, Wo, bo):
            Bq, Lq, Dm = q.shape
            dh = Dm // H
            qh = (q @ Wq + bq).reshape(Bq, Lq, H, dh)
            kh = (k @ Wk + bk).reshape(Bq, -1, H, dh)
            vh = (v @ Wv + bv).reshape(Bq, -1, H, dh)
            scores = jnp.einsum('bqhd,bkhd->bhqk', qh, kh) / jnp.asarray(np.sqrt(dh), q.dtype)
            attn = jax.nn.softmax(scores, axis=-1)
            out = jnp.einsum('bhqk,bkhd->bqhd', attn, vh).reshape(Bq, Lq, Dm)
            return out @ Wo + bo
        Bx = x.shape[0]
        q = jnp.broadcast_to(slot_query, (Bx, NS, D))
        o = q + _mha(q, x, x, d_Wq, d_bq, d_Wk, d_bk, d_Wv, d_bv, d_Wo, d_bo)
        os = o.reshape(Bx, E, S, D)
        h = _layernorm(os, e_ln_g[None, :, None, :], e_ln_b[None, :, None, :])
        u = jax.nn.silu(jnp.einsum('besd,edf->besf', h, e_W1) + e_b1[None, :, None, :])
        g = jax.nn.silu(jnp.einsum('besd,edf->besf', h, e_Wg) + e_bg[None, :, None, :])
        y = jnp.einsum('besf,efd->besd', u * g, e_W2) + e_b2[None, :, None, :]
        o = o + y.reshape(Bx, NS, D)
        out = _mha(x, o, o, c_Wq, c_bq, c_Wk, c_bk, c_Wv, c_bv, c_Wo, c_bo)
        return out
    x = L0_attn_hidden_states
    mod = (_silu(L0_c) @ L0_wmod).reshape(L0_c.shape[0], 6, 1, -1)
    sa, ca, ga, sb, cb, gb = (mod[:, 0], mod[:, 1], mod[:, 2], mod[:, 3], mod[:, 4], mod[:, 5])
    ga = (2 * (ga >= 0) - 1) * jnp.maximum(jnp.abs(ga), 0.25)
    gb = (2 * (gb >= 0) - 1) * jnp.maximum(jnp.abs(gb), 0.25)
    h = _layernorm(x, axis=-1) * (1 + ca) + sa
    x = x + ga * _L0_attn_ref(h, L0_attn_in_proj_w, L0_attn_conv_w, L0_attn_conv_b, L0_attn_ln_g, L0_attn_ln_b, L0_attn_fc_w, L0_attn_fc_b, L0_attn_cproj_w, L0_attn_cproj_b, L0_attn_out_w)
    h = _layernorm(x, axis=-1) * (1 + cb) + sb
    x = x + gb * _L0_ffn_ref(h, L0_ffn_slot_query, L0_ffn_d_Wq, L0_ffn_d_Wk, L0_ffn_d_Wv, L0_ffn_d_Wo, L0_ffn_d_bq, L0_ffn_d_bk, L0_ffn_d_bv, L0_ffn_d_bo, L0_ffn_c_Wq, L0_ffn_c_Wk, L0_ffn_c_Wv, L0_ffn_c_Wo, L0_ffn_c_bq, L0_ffn_c_bk, L0_ffn_c_bv, L0_ffn_c_bo, L0_ffn_e_ln_g, L0_ffn_e_ln_b, L0_ffn_e_W1, L0_ffn_e_b1, L0_ffn_e_Wg, L0_ffn_e_bg, L0_ffn_e_W2, L0_ffn_e_b2)
    return x

_drawn_inputs = setup_inputs


def setup_inputs(seed=0):
    import zlib

    import numpy as np

    out = dict(_drawn_inputs(seed))
    spreads = {'L0_attn_ln_g': (1.0, 0.6),
     'L0_attn_ln_b': (0.0, 0.8),
     'L0_attn_fc_b': (0.0, 0.8),
     'L0_attn_cproj_b': (0.0, 0.8),
     'L0_ffn_d_bq': (0.0, 0.8),
     'L0_ffn_d_bk': (0.0, 2.0),
     'L0_ffn_d_bv': (0.0, 0.8),
     'L0_ffn_d_bo': (0.0, 0.8),
     'L0_ffn_c_bq': (0.0, 0.8),
     'L0_ffn_c_bk': (0.0, 2.0),
     'L0_ffn_c_bv': (0.0, 2.0),
     'L0_ffn_c_bo': (0.0, 2.0),
     'L0_ffn_e_ln_g': (1.0, 0.6),
     'L0_ffn_e_ln_b': (0.0, 0.8),
     'L0_ffn_e_b1': (0.0, 0.8),
     'L0_ffn_e_bg': (0.0, 0.8),
     'L0_ffn_e_b2': (0.0, 0.8)}
    factors = {'L0_attn_in_proj_w': 8.0,
     'L0_attn_conv_w': 8.0,
     'L0_attn_conv_b': 8.0,
     'L0_attn_fc_w': 8.0,
     'L0_attn_cproj_w': 8.0,
     'L0_attn_out_w': 6.52,
     'L0_ffn_slot_query': 8.0,
     'L0_ffn_d_Wq': 8.0,
     'L0_ffn_d_Wk': 8.0,
     'L0_ffn_d_Wv': 8.0,
     'L0_ffn_d_Wo': 8.0,
     'L0_ffn_c_Wq': 8.0,
     'L0_ffn_c_Wk': 8.0,
     'L0_ffn_c_Wv': 8.0,
     'L0_ffn_c_Wo': 8.0,
     'L0_ffn_e_W1': 8.0,
     'L0_ffn_e_Wg': 8.0,
     'L0_ffn_e_W2': 8.0}
    for name, (base, spread) in spreads.items():
        noise = np.random.default_rng([zlib.crc32(name.encode()), seed]).standard_normal(out[name].shape)
        drawn = base * np.exp(spread * noise) if base else spread * noise
        out[name] = jnp.asarray(drawn.astype(out[name].dtype))
    for name, factor in factors.items():
        out[name] = (out[name] * factor).astype(out[name].dtype)
    return out
```

```python
from contextlib import ExitStack

import numpy as np

import concourse.bass as bass
from concourse import mybir

F32 = mybir.dt.float32
ALU = mybir.AluOpType
ACT = mybir.ActivationFunctionType
AX_X = mybir.AxisListType.X

P = 128
D = 128
NS = 16
T = 256
TT = T // P
I = 256
IC = I // P
K = 4
CG = 32
G = I // CG
H = 16
DH = D // H
S = 16
HS = H * S
HC = HS // P
HPC = H // HC
F = 512
FC = F // P
Q = 32
EG = P // Q
NG = S // EG
VW = D + 2
EPS = 1e-5
R8 = float(1.0 / np.sqrt(DH))


def columns(parts):
    at, out = 0, {}
    for name, width in parts:
        out[name] = (at, at + width)
        at += width
    return out, at


SETUP_PARTS, SETUP_W = columns([
    ("ident", P), ("c_t", NS), ("slot_t", S), ("vec", 17), ("pad", 3),
    ("wmod", 6 * D), ("w_h", IC * D), ("w_gate_t", I), ("fc_t", IC * D), ("out_t", IC * D), ("cproj", IC * D),
    ("d_wq", D), ("d_wk_t", D), ("d_wv", D), ("d_wo", D), ("c_wq", D), ("c_wo", D),
    ("mask_j", H), ("mask_c", HC * D), ("sel", P)])
LATE_PARTS, LATE_W = columns([
    ("c_wk", D), ("c_wv", D), ("e_g_t", S), ("e_b_t", S), ("e_b2_t", S)])
VEC = {n: i for i, n in enumerate([
    "conv_b0", "conv_b1", "ln_g0", "ln_g1", "ln_b0", "ln_b1", "cproj_b0", "cproj_b1", "fc_b",
    "d_bq", "d_bk", "d_bv", "d_bo", "c_bq", "c_bk", "c_bv", "c_bo"])}


def exists(b):
    return not isinstance(b, int) or 0 <= b < NS


def wait(eng, sem, count):
    if isinstance(count, int):
        count = min(count, NS)
        if count <= 0:
            return
    eng.wait_ge(sem, count)


def wait_alone(eng, sem, count, passed):
    wait(eng, sem, count)
    if not isinstance(count, int):
        eng.sem_inc(passed, 1)


def adaln_block_kernel(nc, x_tok, x_feat, setup_w, conv_w, late_w, e_w1, e_wg, e_w2, e_b1, e_bg, out):
    ctx = ExitStack()
    with ctx:
        def sb(name, *shape):
            return ctx.enter_context(nc.sbuf_tensor(name, [P, *shape], F32))

        def sem(name):
            return ctx.enter_context(nc.semaphore(name))

        x_in = sb("x_in", NS, TT, D)
        xres = sb("xres", NS, T)
        sw = sb("sw", SETUP_W)
        lw = sb("lw", LATE_W)
        conv_bd = sb("conv_bd", IC, K, P)
        w1 = sb("w1", S, F)
        wg = sb("wg", S, F)
        w2 = sb("w2", S, FC, D)
        b1, bg = (x_in[:, 8 * i:8 * i + 8, :, :].rearrange("p b i d -> p (b i d)")
                  .rearrange("p (g f) -> p g f", g=NG) for i in range(2))

        def carver(base):
            at = [0]

            def carve(*shape):
                a, b = at[0], at[0] + int(np.prod(shape))
                at[0] = b
                names = " ".join("abc"[:len(shape)])
                return base[:, a:b].rearrange(f"p ({names}) -> p {names}", **dict(zip("abc", shape)))
            return carve

        def part(name):
            a, b = SETUP_PARTS[name]
            return sw[:, a:b]

        def late(name):
            a, b = LATE_PARTS[name]
            return lw[:, a:b]

        def vec(name):
            a = SETUP_PARTS["vec"][0] + VEC[name]
            return sw[:, a:a + 1]

        ident = part("ident")
        w_h = part("w_h").rearrange("p (c d) -> p c d", c=IC)
        w_gate = part("w_gate_t").rearrange("p (c d) -> p c d", c=IC)
        fc_t = part("fc_t").rearrange("p (c d) -> p c d", c=IC)
        out_t = part("out_t").rearrange("p (c d) -> p c d", c=IC)
        cproj = part("cproj").rearrange("p (c d) -> p c d", c=IC)
        wmod = part("wmod").rearrange("p (m d) -> p m d", m=6)
        mask_j = part("mask_j")
        mask_c = part("mask_c").rearrange("p (c j) -> p c j", c=HC)
        sel = part("sel")

        c_tanh = sb("c_tanh", NS)
        c_silu = sb("c_silu", NS)
        mod = sb("mod", 6, NS)
        gate_sign = sb("gate_sign", 2, NS)
        gate_bias = sb("gate_bias", 2, NS)
        conv_m = sb("conv_m", IC, K, P)
        conv_bh = sb("conv_bh", IC)
        fc_g = sb("fc_g", IC, D)
        fc_c = sb("fc_c", IC, D)
        z_bias = sb("z_bias", 2)
        out_m = sb("out_m", D)
        slot_q = sb("slot_q", S)
        slot_bd = sb("slot_bd", H, S)
        key_q = sb("key_q", HC, P)
        key_b = sb("key_b", HC)
        slot_o = sb("slot_o", S)
        bias_o = sb("bias_o", 3)
        bq8 = sb("bq8", 1)
        means = sb("means", P)
        eps = sb("eps", TT)
        half_neg = sb("half_neg", TT)

        st1, mv1, ve1, rs1 = sb("st1", TT, 6), sb("mv1", TT, 2), sb("ve1", TT), sb("rs1", TT)
        sth, mvh, veh, rsh = sb("sth", TT, 6), sb("mvh", TT, 2), sb("veh", TT), sb("rsh", TT)
        st2, mv2, ve2, rs2 = sb("st2", TT, 6), sb("mv2", TT, 2), sb("ve2", TT), sb("rs2", TT)
        work = sb("work", 4096)
        carve = carver(work)
        n1 = carve(TT, D)
        hn_t = sb("hn_t", K - 1 + T)
        g_tanh = carve(IC, T)
        g_silu2 = carve(IC, T)
        h = carve(IC, T)
        y_s = carve(TT, D)
        z = carve(T)
        z_tanh = carve(T)
        z_silu2 = carve(T)
        out_g = carve(T)
        x1 = carve(T)
        n2 = carve(TT, D)
        h2_t = carve(T)
        q_t = sb("q_t", NS, T)
        val = sb("val", TT, VW)
        mx = sb("mx", HC)
        mxb = sb("mxb", HC)
        ebias = sb("ebias", HC)
        prob = sb("prob", HC, T)
        prob_t = sb("prob_t", TT, HS)
        rsum = sb("rsum", HC)
        att_m = sb("att_m", HC, D)
        att_t = sb("att_t", NS, S)
        o_t = sb("o_t", NS, S)
        st3, mv3, ve3, rs3 = sb("st3", 2, 6), sb("mv3", 2, 2), sb("ve3", 2), sb("rs3", 2)
        n3 = sb("n3", 2, D)
        ng3 = sb("ng3", NS, S)
        he_t = sb("he_t", S, Q)
        carve = carver(work)
        ub, gb_, us, gs = (carve(2, F) for _ in range(4))
        ug = conv_bd[:, :, :, :].rearrange("p c k o -> p c (k o)")
        ug_t = conv_m
        ye = sb("ye", 2, D)
        o2_t = sb("o2_t", NS, S)
        k2_t = sb("k2_t", NS, S)
        carve = carver(work)
        q_s = carve(T)
        k2_bd = carve(H, S)
        v2t_bd = carve(H, S)
        v2_t = carve(NS, S)
        v2w = carve(HC, D)
        e2 = carve(TT, HS)
        p2 = carve(TT, HS)
        y2g = carve(T)
        mx2 = sb("mx2", TT, H)
        sum2 = sb("sum2", TT, H)
        rsum2 = sb("rsum2", TT, H)
        s2_rows, p2_t = prob, prob_t

        ps = ctx.enter_context(nc.psum_tensor("ps", [P, 8, 512], F32))

        def bank(n, *shape):
            width = int(np.prod(shape))
            v = ps[:, n, 0:width]
            if len(shape) == 2:
                v = v.rearrange("p (a b) -> p a b", a=shape[0])
            return v

        gate_ps = bank(0, IC, T)
        conv_ps = bank(1, IC, T)
        hT_ps = bank(2, TT, I)
        pT_ps = bank(2, TT, HS)
        s_ps = bank(3, HC, T)
        av_ps = bank(3, HC, VW)
        y_ps = bank(4, TT, D)
        out_ps = bank(4, T)
        yT_ps = bank(5, T)
        hn_ps = bank(5, T)
        x1_ps = bank(6, TT, D)
        n2_ps = bank(6, T)
        q_ps = ps[:, 7, 0:T]
        v_ps = ps[:, 7, T:2 * T].rearrange("p (a b) -> p a b", a=TT)
        at_ps = bank(7, P)

        setup_in = sem("setup_in")
        conv_in = sem("conv_in")
        x_in_sem = [sem(f"x_in{i}") for i in range(4)]
        xres_in = sem("xres_in")
        late_in = sem("late_in")
        expert_in = sem("expert_in")
        zeroed = sem("zeroed")
        (c_tanh_ok, c_ready, conv_m_mm, slot_q_mm, mod_mm, fc_g_ok, fc_mean_mm, slot_bd_ok, key_q_mm, out_m_mm,
         bias_mm, dve_chain) = (sem(n) for n in [
             "c_tanh_ok", "c_ready", "conv_m_mm", "slot_q_mm", "mod_mm", "fc_g_ok", "fc_mean_mm", "slot_bd_ok",
             "key_q_mm", "out_m_mm", "bias_mm", "dve_chain"])
        setup_done_dve = sem("setup_done_dve")
        setup_done_act = sem("setup_done_act")
        pool_ready = sem("pool_ready")
        ev = {n: sem(n) for n in [
            "st1_ok", "mv1_ok", "ve1_ok", "rs1_ok", "n1_ok", "hn_mm", "hn_ok", "gate_mm", "gtanh_ok", "gsilu_ok",
            "conv_mm", "h_ok", "hT_mm", "y_mm", "sth_ok", "mvh_ok", "veh_ok", "rsh_ok", "ys_ok", "yT_mm", "ztanh_ok",
            "zsilu_ok", "out_mm", "outg_ok", "x1_ok", "x1_kept", "x1_mm", "st2_ok", "mv2_ok", "ve2_ok", "rs2_ok", "n2_ok",
            "n2_mm", "h2_ok", "s_mm", "mx_ok", "mxb_ok", "ebias_ok", "prob_ok", "qv_mm", "qv_ok", "pT_mm", "pT_ok",
            "av_mm", "rsum_ok", "attm_ok", "at_mm", "at_ok"]}
        o_mm, o_ok, oT_mm, e_chain, e_pool, eT_mm, he_ok = (sem(n) for n in [
            "o_mm", "o_ok", "oT_mm", "e_chain", "e_pool", "eT_mm", "he_ok"])
        u_mm, ub_ok, us_ok, ug_ok, ugT_mm, ugT_ok, ye_mm, ye_ok, yeT_mm, o2_ok, k2_mm, k2_ok = (sem(n) for n in [
            "u_mm", "ub_ok", "us_ok", "ug_ok", "ugT_mm", "ugT_ok", "ye_mm", "ye_ok", "yeT_mm", "o2_ok", "k2_mm",
            "k2_ok"])
        f = {n: sem("f_" + n) for n in [
            "k2bd_ok", "qs_ok", "v2bd_ok", "v2w_mm", "v2w_ok", "s2_mm", "mx2_ok", "s2_half", "s2_ok", "e2_half", "e2_ok", "sum2_ok", "rsum2_ok",
            "p2_half", "p2_ok", "p2T_mm", "p2T_ok", "y2_mm", "y2g_ok", "xo_ok"]}
        v2_mm, v2_ok = sem("v2_mm"), sem("v2_ok")
        stored = sem("stored")
        act_passed, dve_passed, pool_passed = sem("act_passed"), sem("dve_passed"), sem("pool_passed")

        block = ctx.enter_context(nc.Block())

        FIRST, LAST = -2, NS + 1
        LOOP = (2, NS - 2)
        LOOP2 = (3, NS - 1)
        LAST2 = NS + 1

        @block.sync
        def _(sp):
            sp.dma_start(sw[:, :], setup_w).then_inc(setup_in, 16)
            sp.dma_start(x_in[:, 0:4, :, :], x_tok[:, 0:4, :, :]).then_inc(x_in_sem[0], 16)
            sp.wait_ge(zeroed, 1)
            for g in range(G // IC):
                r = slice(g * CG, (g + 1) * CG)
                for c in range(IC):
                    sp.dma_start(conv_bd[r, c, :, r], conv_w[:, c, g, :, :]).then_inc(conv_in, 16)
            for i in range(1, 4):
                sp.dma_start(x_in[:, 4 * i:4 * i + 4, :, :], x_tok[:, 4 * i:4 * i + 4, :, :]).then_inc(x_in_sem[i], 16)
            sp.dma_start(xres[:, :, :], x_feat).then_inc(xres_in, 16)
            sp.dma_start(lw[:, :], late_w).then_inc(late_in, 16)
            for e in range(0, S, 4):
                sp.dma_start(w1[:, e:e + 4, :], e_w1[:, e:e + 4, :]).then_inc(expert_in, 16)
                sp.dma_start(wg[:, e:e + 4, :], e_wg[:, e:e + 4, :]).then_inc(expert_in, 16)
                sp.dma_start(w2[:, e:e + 4, :, :], e_w2[:, e:e + 4, :, :]).then_inc(expert_in, 16)
            sp.wait_ge(ev["n1_ok"], NS)
            for src, dst in ((e_b1, b1), (e_bg, bg)):
                for j in range(EG):
                    sp.dma_start(dst[Q * j:Q * j + Q, :, :],
                                 src.rearrange("(g j) f -> j g f", j=EG)[j:j + 1].broadcast_to([Q, NG, F])
                                 ).then_inc(expert_in, 16)
            with sp.Fori(0, NS) as t:
                sp.wait_ge(f["xo_ok"], t + 1)
                sp.dma_start(out[:, bass.ds(t, 1), :], xres[:, bass.ds(t, 1), :]).then_inc(stored, 16)
            sp.wait_ge(stored, 16 * NS)
        EXPERT_LOADS = 16 * (2 * EG + 3 * (S // 4))

        @block.gpsimd
        def _(pool):
            nc.gpsimd.memset(conv_bd[:, :, :, :], 0.0).then_inc(zeroed, 1)
            nc.gpsimd.memset(eps[:, :], EPS)
            nc.gpsimd.memset(half_neg[:, :], -0.5)
            nc.gpsimd.memset(hn_t[:, 0:K - 1], 0.0)
            nc.gpsimd.memset(val[:, :, D:VW], 1.0)
            nc.gpsimd.memset(he_t[:, :, :], 0.0)
            nc.gpsimd.memset(means[:, :], 1.0 / I).then_inc(pool_ready, 1)

            def rsqrt(mv, ve, rs, mv_ok, ve_ok, rs_ok, b):
                wait(pool, mv_ok, b + 1)
                nc.gpsimd.tensor_tensor(ve[:, :], mv[:, :, 1], eps[:, :], ALU.add).then_inc(ve_ok, 1)
                wait(pool, ve_ok, b + 1)
                nc.gpsimd.tensor_tensor(rs[:, :], ve[:, :], half_neg[:, :], ALU.pow).then_inc(rs_ok, 1)

            def slot(t):
                if exists(t):
                    rsqrt(mvh, veh, rsh, ev["mvh_ok"], ev["veh_ok"], ev["rsh_ok"], t)
                if exists(t + 2):
                    rsqrt(mv1, ve1, rs1, ev["mv1_ok"], ev["ve1_ok"], ev["rs1_ok"], t + 2)
                if exists(t):
                    wait_alone(pool, ev["outg_ok"], t + 1, pool_passed)
                    xs = xres[:, bass.ds(t, 1), :].rearrange("p a t -> p (a t)")
                    nc.gpsimd.tensor_tensor(x1[:, :], xs, out_g[:, :], ALU.add).then_inc(ev["x1_ok"], 1)
                    wait_alone(pool, ev["x1_ok"], t + 1, pool_passed)
                    nc.gpsimd.tensor_copy(xs, x1[:, :]).then_inc(ev["x1_kept"], 1)
                if exists(t):
                    rsqrt(mv2, ve2, rs2, ev["mv2_ok"], ev["ve2_ok"], ev["rs2_ok"], t)

            pool.wait_ge(pool_ready, 1)
            pool.wait_ge(xres_in, 16)
            for t in range(FIRST, LOOP[0]):
                slot(t)
            with pool.Fori(*LOOP) as t:
                slot(t)
            for t in range(LOOP[1], LAST + 1):
                slot(t)

            pool.wait_ge(e_chain, 2)
            nc.gpsimd.tensor_tensor(ve3[:, :], mv3[:, :, 1], eps[:, :], ALU.add).then_inc(e_pool, 1)
            pool.wait_ge(e_pool, 1)
            nc.gpsimd.tensor_tensor(rs3[:, :], ve3[:, :], half_neg[:, :], ALU.pow).then_inc(e_pool, 1)

            def keys(t):
                wait_alone(pool, f["s2_mm"], t, pool_passed)
                kb = k2_t[:, bass.ds(t, 1), :].broadcast_to([P, H, S])
                nc.gpsimd.tensor_tensor(k2_bd[:, :, :], kb, mask_j.unsqueeze(2).broadcast_to([P, H, S]),
                                        ALU.mult).then_inc(f["k2bd_ok"], 1)

            def values(t):
                wait_alone(pool, f["v2w_mm"], t, pool_passed)
                vb = v2_t[:, bass.ds(t, 1), :].broadcast_to([P, H, S])
                nc.gpsimd.tensor_tensor(v2t_bd[:, :, :], vb, mask_j.unsqueeze(2).broadcast_to([P, H, S]),
                                        ALU.mult).then_inc(f["v2bd_ok"], 1)

            def residual2(t):
                wait_alone(pool, f["y2g_ok"], t + 1, pool_passed)
                xs = xres[:, bass.ds(t, 1), :].rearrange("p a t -> p (a t)")
                nc.gpsimd.tensor_tensor(xs, xs, y2g[:, :], ALU.add).then_inc(f["xo_ok"], 1)

            def slot2(t):
                if exists(t + 1):
                    keys(t + 1)
                if exists(t):
                    values(t)
                if exists(t - 2):
                    residual2(t - 2)

            pool.wait_ge(k2_ok, 1)
            pool.wait_ge(v2_ok, 1)
            keys(0)
            for t in range(0, LOOP2[0]):
                slot2(t)
            with pool.Fori(*LOOP2) as t:
                slot2(t)
            for t in range(LOOP2[1], LAST2 + 1):
                slot2(t)

        @block.scalar
        def _(act):
            act.wait_ge(setup_in, 16)
            nc.scalar.activation(c_tanh[:, :], part("c_t"), ACT.Tanh, scale=0.5).then_inc(c_tanh_ok, 1)
            for c in range(IC):
                act.wait_ge(conv_m_mm, 1 + c)
                nc.scalar.mul(conv_m[:, c, :, :], bank(1 + c, K, P), 0.5)
            act.wait_ge(key_q_mm, 1)
            nc.scalar.copy(key_q[:, :, :], bank(6, HC, P))
            act.wait_ge(out_m_mm, 1)
            nc.scalar.mul(out_m[:, :], bank(5, D), 0.5).then_inc(setup_done_act, 1)
            act.wait_ge(setup_done_dve, 1)

            def modulated(dst, src, scale_at, shift_at, b):
                return nc.scalar.activation(dst, src, ACT.Identity, bias=mod[:, shift_at, bass.ds(b, 1)],
                                            scale=mod[:, scale_at, bass.ds(b, 1)])

            def slot(t):
                if exists(t - 2):
                    wait_alone(act, ev["at_mm"], t - 1, act_passed)
                    nc.scalar.copy(att_t[:, bass.ds(t - 2, 1), :].rearrange("p a s -> p (a s)"),
                                   at_ps[:, 0:S]).then_inc(ev["at_ok"], 1)
                if exists(t):
                    wait(act, ev["rsh_ok"], t + 1)
                    wait(act, ev["y_mm"], t + 1)
                    wait(act, ev["yT_mm"], t)
                    for i in range(TT):
                        ins = nc.scalar.activation(y_s[:, i, :], y_ps[:, i, :], ACT.Identity, scale=rsh[:, i:i + 1])
                    ins.then_inc(ev["ys_ok"], 1)
                if exists(t + 1):
                    wait(act, ev["gate_mm"], t + 2)
                    nc.scalar.activation(g_tanh[:, :, :], gate_ps, ACT.Tanh, scale=0.5).then_inc(ev["gtanh_ok"], 1)
                if exists(t - 1):
                    wait_alone(act, ev["n2_mm"], t, act_passed)
                    modulated(h2_t[:, :], n2_ps, 4, 3, t - 1).then_inc(ev["h2_ok"], 1)
                if exists(t):
                    wait(act, ev["yT_mm"], t + 1)
                    nc.scalar.activation(z[:, :], yT_ps, ACT.Identity, bias=z_bias[:, 0:1])
                    nc.scalar.activation(z_tanh[:, :], yT_ps, ACT.Tanh, bias=z_bias[:, 1:2],
                                         scale=0.5).then_inc(ev["ztanh_ok"], 1)
                if exists(t):
                    wait_alone(act, ev["out_mm"], t + 1, act_passed)
                    nc.scalar.activation(out_g[:, :], out_ps, ACT.Identity, bias=gate_bias[:, 0, bass.ds(t, 1)],
                                         scale=mod[:, 2, bass.ds(t, 1)]).then_inc(ev["outg_ok"], 1)
                if exists(t - 1):
                    wait(act, ev["ebias_ok"], t)
                    for c in range(HC):
                        ins = nc.scalar.activation(prob[:, c, :], s_ps[:, c, :], ACT.Exp, bias=ebias[:, c:c + 1])
                    ins.then_inc(ev["prob_ok"], 1)
                if exists(t - 1):
                    wait_alone(act, ev["qv_mm"], t, act_passed)
                    nc.scalar.copy(val[:, :, 0:D], v_ps)
                    nc.scalar.activation(q_t[:, bass.ds(t - 1, 1), :].rearrange("p a t -> p (a t)"), q_ps, ACT.Identity,
                                         bias=bq8[:, :], scale=R8).then_inc(ev["qv_ok"], 1)
                if exists(t - 1):
                    wait(act, ev["pT_mm"], t)
                    nc.scalar.copy(prob_t[:, :, :], pT_ps).then_inc(ev["pT_ok"], 1)
                if exists(t + 2):
                    wait_alone(act, ev["hn_mm"], t + 3, act_passed)
                    modulated(hn_t[:, K - 1:K - 1 + T], hn_ps, 1, 0, t + 2).then_inc(ev["hn_ok"], 1)

            for t in range(FIRST, LOOP[0]):
                slot(t)
            with act.Fori(*LOOP) as t:
                slot(t)
            for t in range(LOOP[1], LAST + 1):
                slot(t)

            def silus(g):
                act.wait_ge(ub_ok, 2 * g + 1)
                nc.scalar.activation(us[:, g % 2, :], ub[:, g % 2, :], ACT.Silu)
                act.wait_ge(ub_ok, 2 * g + 2)
                if g >= 2:
                    act.wait_ge(ug_ok, g - 1)
                nc.scalar.activation(gs[:, g % 2, :], gb_[:, g % 2, :], ACT.Silu).then_inc(us_ok, 1)

            def hidden_t(g):
                act.wait_ge(ugT_mm, g + 1)
                if g >= 2:
                    act.wait_ge(ye_mm, g - 1)
                nc.scalar.copy(ug_t[:, g % 2, :, :], bank(2, FC, P)).then_inc(ugT_ok, 1)

            def outputs(g):
                act.wait_ge(ye_mm, g + 1)
                nc.scalar.copy(ye[:, g % 2, :], bank(3, D)).then_inc(ye_ok, 1)

            for g in range(NG + 2):
                if g < NG:
                    silus(g)
                if 1 <= g < NG + 1:
                    hidden_t(g - 1)
                if g >= 2:
                    outputs(g - 2)

            halves2 = (("s2_half", "p2_half", "e2_half"), ("s2_ok", "p2_ok", "e2_ok"))

            def queries2(b):
                wait_alone(act, f["s2_mm"], b, act_passed)
                nc.scalar.copy(q_s[:, :], q_t[:, bass.ds(b, 1), :].rearrange("p a t -> p (a t)")
                               ).then_inc(f["qs_ok"], 1)

            def slot2(t):
                if exists(t - 2):
                    wait(act, f["p2T_mm"], t - 1)
                    nc.scalar.copy(p2_t[:, :, :], bank(1, HC, T)).then_inc(f["p2T_ok"], 1)
                if exists(t + 1):
                    queries2(t + 1)
                if exists(t):
                    for i in range(TT):
                        shifted, used, made = halves2[i]
                        wait(act, f[shifted], t + 1)
                        wait(act, f[used], t)
                        nc.scalar.activation(e2[:, i, :], s2_rows[:, i, :], ACT.Exp).then_inc(f[made], 1)
                if exists(t - 1):
                    wait(act, f["y2_mm"], t - 1)
                    wait(act, f["v2w_mm"], t)
                    nc.scalar.copy(v2w[:, :, :], bank(5, HC, D)).then_inc(f["v2w_ok"], 1)
                if exists(t - 2):
                    wait_alone(act, f["y2_mm"], t - 1, act_passed)
                    wait_alone(act, f["xo_ok"], t - 2, act_passed)
                    nc.scalar.activation(y2g[:, :], bank(4, T), ACT.Identity, bias=gate_bias[:, 1, bass.ds(t - 2, 1)],
                                         scale=mod[:, 5, bass.ds(t - 2, 1)]).then_inc(f["y2g_ok"], 1)

            queries2(0)
            for t in range(0, LOOP2[0]):
                slot2(t)
            with act.Fori(*LOOP2) as t:
                slot2(t)
            for t in range(LOOP2[1], LAST2 + 1):
                slot2(t)

        @block.tensor
        def _(pe):
            def mm(dst, lhs, rhs, first=True, last=True):
                return nc.tensor.matmul(dst, lhs, rhs, start=first, stop=last)

            def flip(dst, src):
                return nc.tensor.transpose(dst, src, ident)

            pe.wait_ge(setup_in, 16)
            mm(bank(7, S), part("d_wq"), part("slot_t")).then_inc(slot_q_mm, 1)
            pe.wait_ge(conv_in, 16 * G)
            for c in range(IC):
                mm(ps[:, 1 + c, :], w_h[:, c, :], conv_bd[:, c, :, :]).then_inc(conv_m_mm, 1)
            pe.wait_ge(c_ready, 1)
            for m in range(6):
                ins = mm(ps[:, 0, m * NS:(m + 1) * NS], wmod[:, m, :], c_silu[:, :])
            ins.then_inc(mod_mm, 1)
            pe.wait_ge(fc_g_ok, 1)
            pe.wait_ge(pool_ready, 1)
            for c in range(IC):
                ins = mm(bank(3, D), means[:, :], fc_g[:, c, :], c == 0, c == IC - 1)
            ins.then_inc(fc_mean_mm, 1)
            pe.wait_ge(slot_bd_ok, 1)
            mm(bank(6, HS), part("d_wk_t"), slot_bd[:, :, :]).then_inc(key_q_mm, 1)
            for c in range(IC):
                ins = mm(bank(5, D), cproj[:, c, :], out_t[:, c, :], c == 0, c == IC - 1)
            ins.then_inc(out_m_mm, 1)
            for c in range(IC):
                mm(ps[:, 4, 0:1], fc_t[:, c, :], vec(f"ln_b{c}"), c == 0, c == IC - 1)
            for c in range(IC):
                mm(ps[:, 4, 1:2], out_t[:, c, :], vec(f"cproj_b{c}"), c == 0, c == IC - 1)
            for c in range(HC):
                mm(ps[:, 4, 2 + c:3 + c], slot_bd[:, c * HPC:(c + 1) * HPC, :], vec("d_bk"))
            mm(ps[:, 4, 4:5], part("d_wo"), vec("d_bv"))
            mm(ps[:, 4, 5:6], part("c_wo"), vec("c_bv")).then_inc(bias_mm, 1)
            pe.wait_ge(setup_done_act, 1)
            pe.wait_ge(setup_done_dve, 1)

            def norm_to_features(b):
                wait(pe, ev["n1_ok"], b + 1)
                wait(pe, ev["ztanh_ok"], b - 1)
                for i in range(TT):
                    ins = flip(hn_ps[:, i * P:(i + 1) * P], n1[:, i, :])
                ins.then_inc(ev["hn_mm"], 1)

            def gate(b):
                wait(pe, ev["hn_ok"], b + 1)
                wait(pe, ev["gsilu_ok"], b)
                for c in range(IC):
                    ins = mm(gate_ps[:, c, :], w_gate[:, c, :], hn_t[:, K - 1:K - 1 + T])
                ins.then_inc(ev["gate_mm"], 1)

            def conv(b, c, taps):
                if c == 0 and taps[0] == 0:
                    wait(pe, ev["h_ok"], b)
                for k in taps:
                    ins = mm(conv_ps[:, c, :], conv_m[:, c, k, :], hn_t[:, k:k + T], k == 0, k == K - 1)
                if c == IC - 1 and taps[-1] == K - 1:
                    ins.then_inc(ev["conv_mm"], 1)

            def inner_product(b):
                wait(pe, ev["h_ok"], b + 1)
                wait(pe, ev["pT_ok"], b - 1)
                for i in range(TT):
                    for c in range(IC):
                        ins = flip(hT_ps[:, i, c * P:(c + 1) * P], h[:, c, i * P:(i + 1) * P])
                ins.then_inc(ev["hT_mm"], 1)
                wait(pe, ev["outg_ok"], b)
                for i in range(TT):
                    for c in range(IC):
                        ins = mm(y_ps[:, i, :], h[:, c, i * P:(i + 1) * P], fc_c[:, c, :], c == 0, c == IC - 1)
                ins.then_inc(ev["y_mm"], 1)

            def inner_to_features(b):
                wait(pe, ev["ys_ok"], b + 1)
                wait(pe, ev["hn_ok"], b + 2)
                for i in range(TT):
                    ins = flip(yT_ps[:, i * P:(i + 1) * P], y_s[:, i, :])
                ins.then_inc(ev["yT_mm"], 1)

            def project_out(b):
                wait(pe, ev["zsilu_ok"], b + 1)
                for c in range(IC):
                    mm(out_ps, out_t[:, c, :], h[:, c, :], c == 0, False)
                mm(out_ps, out_m[:, :], z_silu2[:, :], False, True).then_inc(ev["out_mm"], 1)

            def residual_to_tokens(b):
                wait(pe, ev["x1_ok"], b + 1)
                wait(pe, ev["h2_ok"], b)
                for i in range(TT):
                    ins = flip(x1_ps[:, i, :], x1[:, i * P:(i + 1) * P])
                ins.then_inc(ev["x1_mm"], 1)

            def norm2_to_features(b):
                wait(pe, ev["n2_ok"], b + 1)
                for i in range(TT):
                    ins = flip(n2_ps[:, i * P:(i + 1) * P], n2[:, i, :])
                ins.then_inc(ev["n2_mm"], 1)

            def scores(b):
                wait(pe, ev["h2_ok"], b + 1)
                wait(pe, ev["attm_ok"], b)
                for c in range(HC):
                    ins = mm(s_ps[:, c, :], key_q[:, c, :], h2_t[:, :])
                ins.then_inc(ev["s_mm"], 1)

            def queries_values(b):
                wait(pe, ev["at_ok"], b)
                mm(q_ps, part("c_wq"), h2_t[:, :])
                for i in range(TT):
                    ins = mm(v_ps[:, i, :], h2_t[:, i * P:(i + 1) * P], part("d_wv"))
                ins.then_inc(ev["qv_mm"], 1)

            def prob_to_tokens(b):
                wait(pe, ev["prob_ok"], b + 1)
                wait(pe, ev["sth_ok"], b + 2)
                for i in range(TT):
                    for c in range(HC):
                        ins = flip(pT_ps[:, i, c * P:(c + 1) * P], prob[:, c, i * P:(i + 1) * P])
                ins.then_inc(ev["pT_mm"], 1)

            def attend(b):
                wait(pe, ev["pT_ok"], b + 1)
                wait(pe, ev["qv_ok"], b + 1)
                for c in range(HC):
                    for i in range(TT):
                        ins = mm(av_ps[:, c, 0:D + 1], prob_t[:, i, c * P:(c + 1) * P], val[:, i, 0:D + 1],
                                 i == 0, i == TT - 1)
                ins.then_inc(ev["av_mm"], 1)

            def gather_heads(b):
                wait(pe, ev["attm_ok"], b + 1)
                wait(pe, ev["qv_ok"], b + 1)
                for c in range(HC):
                    ins = mm(at_ps, att_m[:, c, :], sel, c == 0, c == HC - 1)
                ins.then_inc(ev["at_mm"], 1)

            def slot(t):
                if exists(t):
                    inner_product(t)
                if exists(t - 2):
                    gather_heads(t - 2)
                if exists(t + 1):
                    gate(t + 1)
                    conv(t + 1, 0, range(0, K // 2))
                if exists(t - 1):
                    norm2_to_features(t - 1)
                if exists(t):
                    inner_to_features(t)
                if exists(t + 1):
                    conv(t + 1, 0, range(K // 2, K))
                if exists(t - 1):
                    scores(t - 1)
                if exists(t):
                    project_out(t)
                if exists(t - 1):
                    queries_values(t - 1)
                if exists(t + 1):
                    conv(t + 1, 1, range(0, K // 2))
                if exists(t):
                    residual_to_tokens(t)
                if exists(t - 1):
                    prob_to_tokens(t - 1)
                if exists(t + 1):
                    conv(t + 1, 1, range(K // 2, K))
                if exists(t - 1):
                    attend(t - 1)
                if exists(t + 2):
                    norm_to_features(t + 2)

            for t in range(FIRST, LOOP[0]):
                slot(t)
            with pe.Fori(*LOOP) as t:
                slot(t)
            for t in range(LOOP[1], LAST + 1):
                slot(t)

            pe.wait_ge(ev["at_ok"], NS)
            pe.wait_ge(late_in, 16)
            pe.wait_ge(expert_in, EXPERT_LOADS)
            mm(bank(0, NS * S), part("d_wo"), att_t[:, :, :]).then_inc(o_mm, 1)
            pe.wait_ge(o_ok, 1)
            for i in range(2):
                ins = flip(ps[:, 1, i * P:(i + 1) * P], o_t[:, i * NS // 2:(i + 1) * NS // 2, :])
            ins.then_inc(oT_mm, 1)
            pe.wait_ge(e_chain, 3)
            for i in range(2):
                ins = flip(ps[:, 2, i * P:(i + 1) * P], n3[:, i, :])
            ins.then_inc(eT_mm, 1)
            pe.wait_ge(he_ok, 1)

            def hidden(g):
                for n, w in ((4, w1), (6, wg)):
                    if g >= 2:
                        pe.wait_ge(ub_ok, 2 * (g - 2) + (1 if n == 4 else 2))
                    for j in range(EG):
                        ins = mm(ps[Q * j:Q * j + Q, n + g % 2, :], he_t[:, EG * g + j, :], w[:, EG * g + j, :])
                    ins.then_inc(u_mm, 1)

            def hidden_to_rows(g):
                pe.wait_ge(ug_ok, g + 1)
                if g >= 1:
                    pe.wait_ge(ugT_ok, g)
                for k in range(FC):
                    ins = flip(ps[:, 2, k * P:(k + 1) * P], ug[:, g % 2, k * P:(k + 1) * P])
                ins.then_inc(ugT_mm, 1)

            def hidden_product(g):
                pe.wait_ge(ugT_ok, g + 1)
                if g >= 1:
                    pe.wait_ge(ye_ok, g)
                for k in range(FC):
                    for j in range(EG):
                        ins = mm(ps[Q * j:Q * j + Q, 3, 0:D], ug_t[:, g % 2, k, Q * j:Q * j + Q],
                                 w2[:, EG * g + j, k, :], k == 0, k == FC - 1)
                ins.then_inc(ye_mm, 1)

            def to_slots(g):
                pe.wait_ge(ye_ok, g + 1)
                if g >= 2:
                    pe.wait_ge(o2_ok, g - 1)
                flip(ps[:, g % 2, 0:P], ye[:, g % 2, :]).then_inc(yeT_mm, 1)

            for g in range(NG + 3):
                if g < NG:
                    hidden(g)
                if 2 <= g < NG + 2:
                    hidden_product(g - 2)
                if 1 <= g < NG + 1:
                    hidden_to_rows(g - 1)
                if 3 <= g < NG + 3:
                    to_slots(g - 3)
            pe.wait_ge(o2_ok, NG)
            mm(bank(4, NS * S), late("c_wk"), o2_t[:, :, :]).then_inc(k2_mm, 1)
            mm(bank(5, NS * S), late("c_wv"), o2_t[:, :, :]).then_inc(v2_mm, 1)
            pe.wait_ge(v2_ok, 1)

            def scores2(b):
                wait(pe, f["k2bd_ok"], b + 1)
                wait(pe, f["qs_ok"], b + 1)
                wait(pe, f["s2_ok"], b)
                for i in range(TT):
                    ins = mm(ps[:, 0, i * HS:(i + 1) * HS], q_s[:, i * P:(i + 1) * P], k2_bd[:, :, :])
                ins.then_inc(f["s2_mm"], 1)

            def probs2_to_rows(b):
                wait(pe, f["p2_ok"], b + 1)
                wait(pe, f["p2T_ok"], b)
                for c in range(HC):
                    for i in range(TT):
                        ins = flip(ps[:, 1, c * T + i * P:c * T + (i + 1) * P], p2[:, i, c * P:(c + 1) * P])
                ins.then_inc(f["p2T_mm"], 1)

            def values2(b):
                wait(pe, f["v2bd_ok"], b + 1)
                wait(pe, f["v2w_ok"], b)
                for c in range(HC):
                    ins = mm(ps[:, 5, c * D:(c + 1) * D], v2t_bd[:, c * HPC:(c + 1) * HPC, :], part("c_wo"))
                ins.then_inc(f["v2w_mm"], 1)

            def outputs2(b):
                wait(pe, f["p2T_ok"], b + 1)
                wait(pe, f["v2w_ok"], b + 1)
                wait(pe, f["y2g_ok"], b)
                for c in range(HC):
                    ins = mm(bank(4, T), v2w[:, c, :], p2_t[:, c, :], c == 0, c == HC - 1)
                ins.then_inc(f["y2_mm"], 1)

            def slot2(t):
                if exists(t):
                    scores2(t)
                if exists(t - 2):
                    probs2_to_rows(t - 2)
                if exists(t - 1):
                    values2(t - 1)
                if exists(t - 2):
                    outputs2(t - 2)

            for t in range(0, LOOP2[0]):
                slot2(t)
            with pe.Fori(*LOOP2) as t:
                slot2(t)
            for t in range(LOOP2[1], LAST2 + 1):
                slot2(t)

        @block.vector
        def _(dve):
            v = nc.vector
            links = [0]

            def chain(ins):
                links[0] += 1
                ins.then_inc(dve_chain, 1)
                dve.wait_ge(dve_chain, links[0])

            def over_samples(x):
                return x.unsqueeze(1).broadcast_to([P, NS, S])

            dve.wait_ge(setup_in, 16)
            for c in range(IC):
                ins = v.tensor_scalar(fc_g[:, c, :], fc_t[:, c, :], vec(f"ln_g{c}"), None, ALU.mult)
            ins.then_inc(fc_g_ok, 1)
            dve.wait_ge(c_tanh_ok, 1)
            chain(v.scalar_tensor_tensor(out=c_silu[:, :], in0=c_tanh[:, :], scalar=1.0, in1=part("c_t"),
                                         op0=ALU.add, op1=ALU.mult))
            v.tensor_scalar(c_silu[:, :], c_silu[:, :], 0.5, None, ALU.mult).then_inc(c_ready, 1)
            dve.wait_ge(slot_q_mm, 1)
            chain(v.tensor_scalar(slot_q[:, :], bank(7, S), vec("d_bq"), R8, ALU.add, ALU.mult))
            v.tensor_tensor(slot_bd[:, :, :], mask_j.unsqueeze(2).broadcast_to([P, H, S]),
                            slot_q[:, :].unsqueeze(1).broadcast_to([P, H, S]), ALU.mult).then_inc(slot_bd_ok, 1)
            v.tensor_scalar(bq8[:, :], vec("c_bq"), R8, None, ALU.mult)
            for c in range(IC):
                v.tensor_scalar(conv_bh[:, c:c + 1], vec(f"conv_b{c}"), 0.5, None, ALU.mult)
            dve.wait_ge(mod_mm, 1)
            chain(v.tensor_copy(mod[:, :, :], bank(0, 6, NS)))
            for m, n in ((2, 0), (5, 1)):
                gate_m, sign = mod[:, m, :], gate_sign[:, n, :]
                chain(v.tensor_scalar(sign, gate_m, -1.0, None, ALU.mult))
                chain(v.tensor_tensor(gate_bias[:, n, :], sign, gate_m, ALU.max))
                chain(v.tensor_scalar(sign, gate_m, 0.0, 2.0, ALU.is_ge, ALU.mult))
                chain(v.tensor_scalar(sign, sign, -1.0, None, ALU.add))
                chain(v.scalar_tensor_tensor(out=gate_m, in0=gate_bias[:, n, :], scalar=0.25, in1=sign,
                                             op0=ALU.max, op1=ALU.mult))
            for m in (1, 4):
                v.tensor_scalar(mod[:, m, :], mod[:, m, :], 1.0, None, ALU.add)
            dve.wait_ge(fc_mean_mm, 1)
            for c in range(IC):
                v.tensor_tensor(fc_c[:, c, :], fc_g[:, c, :], bank(3, D), ALU.subtract)
            dve.wait_ge(bias_mm, 1)
            chain(v.tensor_tensor(z_bias[:, 0:1], ps[:, 4, 0:1], vec("fc_b"), ALU.add))
            v.tensor_scalar(z_bias[:, 1:2], z_bias[:, 0:1], 0.5, None, ALU.mult)
            v.tensor_copy(bias_o[:, 0:1], ps[:, 4, 1:2])
            v.tensor_copy(key_b[:, :], ps[:, 4, 2:4])
            v.tensor_tensor(bias_o[:, 1:2], ps[:, 4, 4:5], vec("d_bo"), ALU.add)
            chain(v.tensor_tensor(bias_o[:, 2:3], ps[:, 4, 5:6], vec("c_bo"), ALU.add))
            v.tensor_scalar(slot_o[:, :], part("slot_t"), bias_o[:, 1:2], None, ALU.add)
            v.tensor_scalar(gate_bias[:, 0, :], mod[:, 2, :], bias_o[:, 0:1], None, ALU.mult)
            v.tensor_scalar(gate_bias[:, 1, :], mod[:, 5, :], bias_o[:, 2:3], None,
                            ALU.mult).then_inc(setup_done_dve, 1)

            def stats(st, mv, srcs, st_ok, mv_ok, b):
                for i in range(TT):
                    ins = v.bn_stats(st[:, i, :], srcs[i])
                ins.then_inc(st_ok, 1)
                wait_alone(dve, st_ok, b + 1, dve_passed)
                for i in range(TT):
                    ins = v.bn_aggr(mv[:, i, :], st[:, i, :])
                ins.then_inc(mv_ok, 1)

            def x_tile(b, i):
                return x_in[:, bass.ds(b, 1), i, :].rearrange("p a d -> p (a d)")

            def slot(t):
                if exists(t - 2):
                    wait(dve, ev["av_mm"], t - 1)
                    v.reciprocal(rsum[:, :], av_ps[:, :, D]).then_inc(ev["rsum_ok"], 1)
                    wait(dve, ev["rsum_ok"], t - 1)
                    for c in range(HC):
                        ins = v.scalar_tensor_tensor(out=att_m[:, c, :], in0=av_ps[:, c, 0:D], scalar=rsum[:, c:c + 1],
                                                     in1=mask_c[:, c, :], op0=ALU.mult, op1=ALU.mult)
                    ins.then_inc(ev["attm_ok"], 1)
                if exists(t):
                    wait(dve, ev["hT_mm"], t + 1)
                    stats(sth, mvh, [hT_ps[:, i, :] for i in range(TT)], ev["sth_ok"], ev["mvh_ok"], t)
                if exists(t - 1):
                    wait(dve, ev["rs2_ok"], t)
                    for i in range(TT):
                        ins = v.tensor_scalar(n2[:, i, :], x1_ps[:, i, :], mv2[:, i, 0:1], rs2[:, i:i + 1],
                                              ALU.subtract, ALU.mult)
                    ins.then_inc(ev["n2_ok"], 1)
                if exists(t + 2):
                    stats(st1, mv1, [x_tile(t + 2, i) for i in range(TT)], ev["st1_ok"], ev["mv1_ok"], t + 2)
                if exists(t + 1):
                    wait(dve, ev["gtanh_ok"], t + 2)
                    v.scalar_tensor_tensor(out=g_silu2[:, :, :], in0=g_tanh[:, :, :], scalar=1.0, in1=gate_ps,
                                           op0=ALU.add, op1=ALU.mult).then_inc(ev["gsilu_ok"], 1)
                if exists(t):
                    wait(dve, ev["ztanh_ok"], t + 1)
                    v.scalar_tensor_tensor(out=z_silu2[:, :], in0=z_tanh[:, :], scalar=1.0, in1=z[:, :],
                                           op0=ALU.add, op1=ALU.mult).then_inc(ev["zsilu_ok"], 1)
                if exists(t - 1):
                    wait(dve, ev["s_mm"], t)
                    v.tensor_reduce(mx[:, :], s_ps, AX_X, ALU.max).then_inc(ev["mx_ok"], 1)
                    wait(dve, ev["mx_ok"], t)
                    v.tensor_tensor(mxb[:, :], mx[:, :], key_b[:, :], ALU.add).then_inc(ev["mxb_ok"], 1)
                    wait(dve, ev["mxb_ok"], t)
                    v.tensor_tensor(ebias[:, :], key_b[:, :], mxb[:, :], ALU.subtract).then_inc(ev["ebias_ok"], 1)
                if exists(t + 2):
                    wait(dve, ev["rs1_ok"], t + 3)
                    wait(dve, ev["hn_mm"], t + 2)
                    for i in range(TT):
                        ins = v.tensor_scalar(n1[:, i, :], x_tile(t + 2, i), mv1[:, i, 0:1], rs1[:, i:i + 1],
                                              ALU.subtract, ALU.mult)
                    ins.then_inc(ev["n1_ok"], 1)
                if exists(t):
                    wait(dve, ev["x1_mm"], t + 1)
                    stats(st2, mv2, [x1_ps[:, i, :] for i in range(TT)], ev["st2_ok"], ev["mv2_ok"], t)
                if exists(t + 1):
                    wait(dve, ev["conv_mm"], t + 2)
                    wait(dve, ev["gsilu_ok"], t + 2)
                    for c in range(IC):
                        ins = v.scalar_tensor_tensor(out=h[:, c, :], in0=conv_ps[:, c, :], scalar=conv_bh[:, c:c + 1],
                                                     in1=g_silu2[:, c, :], op0=ALU.add, op1=ALU.mult)
                    ins.then_inc(ev["h_ok"], 1)

            dve.wait_ge(x_in_sem[0], 16)
            for t in range(FIRST, LOOP[0]):
                slot(t)
            for s_ in x_in_sem[1:]:
                dve.wait_ge(s_, 16)
            with dve.Fori(*LOOP) as t:
                slot(t)
            for t in range(LOOP[1], LAST + 1):
                slot(t)

            dve.wait_ge(late_in, 16)
            dve.wait_ge(o_mm, 1)
            v.tensor_tensor(o_t[:, :, :], bank(0, NS, S), over_samples(slot_o[:, :]), ALU.add).then_inc(o_ok, 1)
            dve.wait_ge(oT_mm, 1)
            for i in range(2):
                ins = v.bn_stats(st3[:, i, :], ps[:, 1, i * P:(i + 1) * P])
            ins.then_inc(e_chain, 1)
            dve.wait_ge(e_chain, 1)
            for i in range(2):
                ins = v.bn_aggr(mv3[:, i, :], st3[:, i, :])
            ins.then_inc(e_chain, 1)
            dve.wait_ge(e_pool, 2)
            for i in range(2):
                ins = v.tensor_scalar(n3[:, i, :], ps[:, 1, i * P:(i + 1) * P], mv3[:, i, 0:1], rs3[:, i:i + 1],
                                      ALU.subtract, ALU.mult)
            ins.then_inc(e_chain, 1)
            v.tensor_tensor(o_t[:, :, :], o_t[:, :, :], over_samples(late("e_b2_t")), ALU.add)
            dve.wait_ge(eT_mm, 1)
            chain(v.tensor_tensor(ng3[:, :, :], bank(2, NS, S), over_samples(late("e_g_t")), ALU.mult))
            v.tensor_tensor(he_t[:, :, 0:NS].rearrange("p s b -> p b s"), ng3[:, :, :], over_samples(late("e_b_t")),
                            ALU.add).then_inc(he_ok, 1)
            dve.wait_ge(expert_in, EXPERT_LOADS)

            def hidden_biases(g):
                for n, (b, dst) in enumerate(((b1, ub), (bg, gb_))):
                    dve.wait_ge(u_mm, 2 * g + n + 1)
                    if g >= 2:
                        dve.wait_ge(us_ok, g - 1)
                    v.tensor_tensor(dst[:, g % 2, :], ps[:, 4 + 2 * n + g % 2, :], b[:, g, :],
                                    ALU.add).then_inc(ub_ok, 1)

            def gated(g):
                dve.wait_ge(us_ok, g + 1)
                if g >= 2:
                    dve.wait_ge(ugT_mm, g - 1)
                v.tensor_tensor(ug[:, g % 2, :], us[:, g % 2, :], gs[:, g % 2, :], ALU.mult).then_inc(ug_ok, 1)

            def add_to_slots(g):
                dve.wait_ge(yeT_mm, g + 1)
                e = slice(EG * g, EG * (g + 1))
                y = ps[:, g % 2, 0:P].rearrange("p (j q) -> p q j", j=EG)[:, 0:NS, :]
                v.tensor_tensor(o2_t[:, :, e], o_t[:, :, e], y, ALU.add).then_inc(o2_ok, 1)

            for g in range(NG + 3):
                if g < NG:
                    hidden_biases(g)
                if 1 <= g < NG + 1:
                    gated(g - 1)
                if g >= 3:
                    add_to_slots(g - 3)
            dve.wait_ge(k2_mm, 1)
            v.tensor_scalar(k2_t[:, :, :], bank(4, NS, S), vec("c_bk"), None, ALU.add).then_inc(k2_ok, 1)

            dve.wait_ge(v2_mm, 1)
            v.tensor_copy(v2_t[:, :, :], bank(5, NS, S)).then_inc(v2_ok, 1)

            def by_head(x):
                return x.rearrange("p (h s) -> p h s", s=S)

            def slot2(t):
                if exists(t - 1):
                    for i, half in enumerate(("e2_half", "e2_ok")):
                        wait(dve, f[half], t)
                        ins = v.tensor_reduce(sum2[:, i, :], by_head(e2[:, i, :]), AX_X, ALU.add)
                    ins.then_inc(f["sum2_ok"], 1)
                if exists(t):
                    wait(dve, f["s2_mm"], t + 1)
                    v.tensor_reduce(mx2[:, :, :], ps[:, 0, :].rearrange("p (a s) -> p a s", s=S), AX_X,
                                    ALU.max).then_inc(f["mx2_ok"], 1)
                if exists(t - 1):
                    wait(dve, f["sum2_ok"], t)
                    v.reciprocal(rsum2[:, :, :], sum2[:, :, :]).then_inc(f["rsum2_ok"], 1)
                if exists(t):
                    wait(dve, f["mx2_ok"], t + 1)
                    for i, half in enumerate(("s2_half", "s2_ok")):
                        v.tensor_tensor(by_head(s2_rows[:, i, :]), by_head(ps[:, 0, i * HS:(i + 1) * HS]),
                                        mx2[:, i, :].unsqueeze(2).broadcast_to([P, H, S]),
                                        ALU.subtract).then_inc(f[half], 1)
                if exists(t - 1):
                    wait(dve, f["p2T_mm"], t - 1)
                    wait(dve, f["rsum2_ok"], t)
                    for i, half in enumerate(("p2_half", "p2_ok")):
                        v.tensor_tensor(by_head(p2[:, i, :]), by_head(e2[:, i, :]),
                                        rsum2[:, i, :].unsqueeze(2).broadcast_to([P, H, S]),
                                        ALU.mult).then_inc(f[half], 1)

            for t in range(0, LOOP2[0]):
                slot2(t)
            with dve.Fori(*LOOP2) as t:
                slot2(t)
            for t in range(LOOP2[1], LAST2 + 1):
                slot2(t)


def kernel(**inputs):
    import concourse.bacc as bacc
    from concourse.bass_utils import run_bass_kernel_spmd

    a = {k: np.asarray(v) for k, v in inputs.items()}

    def attn(name):
        return a["L0_attn_" + name]

    def ffn(name):
        return a["L0_ffn_" + name]

    def by_rows(w):
        return w.reshape(-1, P, w.shape[-1]).transpose(1, 0, 2).reshape(P, -1)

    feature, row = np.arange(D), np.arange(HS)
    mask_j = (feature[:, None] // DH == np.arange(H)).astype(np.float32)
    mask_rows = (row[:, None] // S == feature // DH).astype(np.float32)
    sel = np.zeros((P, P), np.float32)
    sel[:, 0:S] = np.arange(P)[:, None] % S == np.arange(S)

    x = attn("hidden_states")
    w_in = attn("in_proj_w")
    vecs = {
        "conv_b": attn("conv_b"), "ln_g": attn("ln_g"), "ln_b": attn("ln_b"), "cproj_b": attn("cproj_b"),
        "fc_b": attn("fc_b"), "d_bq": ffn("d_bq"), "d_bk": ffn("d_bk"), "d_bv": ffn("d_bv"), "d_bo": ffn("d_bo"),
        "c_bq": ffn("c_bq"), "c_bk": ffn("c_bk"), "c_bv": ffn("c_bv"), "c_bo": ffn("c_bo")}
    vec = np.stack([vecs[n] if n in vecs else vecs[n[:-1]][int(n[-1]) * P:(int(n[-1]) + 1) * P] for n in VEC], 1)
    setup = {
        "ident": np.eye(P, dtype=np.float32), "c_t": a["L0_c"].T, "slot_t": ffn("slot_query")[0].T, "vec": vec,
        "pad": np.zeros((P, 3), np.float32), "wmod": a["L0_wmod"], "w_h": by_rows(w_in[:I]), "w_gate_t": w_in[I:].T,
        "fc_t": by_rows(attn("fc_w").T), "out_t": by_rows(attn("out_w").T), "cproj": by_rows(attn("cproj_w")),
        "d_wq": ffn("d_Wq"), "d_wk_t": ffn("d_Wk").T, "d_wv": ffn("d_Wv"), "d_wo": ffn("d_Wo"),
        "c_wq": ffn("c_Wq"), "c_wo": ffn("c_Wo"), "mask_j": mask_j, "mask_c": by_rows(mask_rows), "sel": sel}
    late = {
        "c_wk": ffn("c_Wk"), "c_wv": ffn("c_Wv"), "e_g_t": ffn("e_ln_g").T, "e_b_t": ffn("e_ln_b").T,
        "e_b2_t": ffn("e_b2").T}
    arrays = {
        "x_tok": x.reshape(NS, TT, P, D).transpose(2, 0, 1, 3),
        "x_feat": x.transpose(2, 0, 1),
        "setup_w": np.concatenate([setup[n] for n in SETUP_PARTS], 1),
        "conv_w": attn("conv_w").reshape(IC, G // IC, CG, CG, K).transpose(3, 0, 1, 4, 2),
        "late_w": np.concatenate([late[n] for n in LATE_PARTS], 1),
        "e_w1": ffn("e_W1").transpose(1, 0, 2),
        "e_wg": ffn("e_Wg").transpose(1, 0, 2),
        "e_w2": ffn("e_W2").reshape(S, FC, P, D).transpose(2, 0, 1, 3),
        "e_b1": ffn("e_b1"),
        "e_bg": ffn("e_bg"),
    }
    arrays = {k: np.ascontiguousarray(v) for k, v in arrays.items()}
    nc = bacc.Bacc("TRN2", target_bir_lowering=False, num_devices=1)
    args = {k: nc.dram_tensor(k, v.shape, F32, kind="ExternalInput").ap() for k, v in arrays.items()}
    out = nc.dram_tensor("out", (P, NS, T), F32, kind="ExternalOutput").ap()
    adaln_block_kernel(nc, **args, out=out)
    r = run_bass_kernel_spmd(nc, [arrays], core_ids=[0])
    return np.ascontiguousarray(r.results[0]["out"].transpose(1, 2, 0))
```

```python
from contextlib import ExitStack

import numpy as np

import concourse.bass as bass
from concourse import mybir

F32 = mybir.dt.float32
ALU = mybir.AluOpType
ACT = mybir.ActivationFunctionType
AX_X = mybir.AxisListType.X

P = 128
D = 128
NS = 16
T = 256
TT = T // P
I = 256
IC = I // P
K = 4
CG = 32
G = I // CG
H = 16
DH = D // H
S = 16
HS = H * S
HC = HS // P
HPC = H // HC
F = 512
FC = F // P
Q = 32
EG = P // Q
NG = S // EG
JC = D // HC
EPS = 1e-5
R8 = float(1.0 / np.sqrt(DH))


def columns(parts):
    at, out = 0, {}
    for name, width in parts:
        out[name] = (at, at + width)
        at += width
    return out, at


SETUP_PARTS, SETUP_W = columns([
    ("ident", P), ("c_t", NS), ("slot_t", S), ("vec", 17), ("pad", 3), ("w_h", IC * D), ("conv_w", IC * K * CG),
    ("wmod", 6 * D), ("d_wq", D), ("w_gate_t", I), ("mask_j", H), ("mask_r", HPC),
    ("fc_t", IC * D), ("out_t", IC * D), ("cproj", IC * D), ("d_wk_t", D), ("d_wv", D), ("d_wo", D), ("c_wq", D),
    ("c_wo", D)])
SETUP_LOADS = (0, SETUP_PARTS["wmod"][0], SETUP_PARTS["fc_t"][0], SETUP_W)
X_LOADS = (0, 2, 4, 10, NS)
LATE_PARTS, LATE_W = columns([
    ("c_wk", D), ("c_wv", D), ("e_g_t", S), ("e_b_t", S), ("e_b2_t", S)])
VEC = {n: i for i, n in enumerate([
    "conv_b0", "conv_b1", "ln_g0", "ln_g1", "ln_b0", "ln_b1", "cproj_b0", "cproj_b1", "fc_b",
    "d_bq", "d_bk", "d_bv", "d_bo", "c_bq", "c_bk", "c_bv", "c_bo"])}


def exists(b):
    return not isinstance(b, int) or 0 <= b < NS


def first(b):
    return isinstance(b, int) and b == 0


def wait(eng, sem, count):
    if isinstance(count, int):
        count = min(count, NS)
        if count <= 0:
            return
    eng.wait_ge(sem, count)


def wait_alone(eng, sem, count, passed):
    wait(eng, sem, count)
    if not isinstance(count, int):
        eng.sem_inc(passed, 1)


def adaln_block_kernel(nc, x_tok, x_feat, setup_w, late_w, e_w1, e_wg, e_w2, e_b1, e_bg, out):
    ctx = ExitStack()
    with ctx:
        def sb(name, *shape):
            return ctx.enter_context(nc.sbuf_tensor(name, [P, *shape], F32))

        def sem(name):
            return ctx.enter_context(nc.semaphore(name))

        x_in = sb("x_in", NS, TT, D)
        xres = sb("xres", NS, T)
        sw = sb("sw", SETUP_W)
        lw = sb("lw", LATE_W)
        conv_bd = sb("conv_bd", IC, K, P)
        w1 = sb("w1", S, F)
        wg = sb("wg", S, F)
        w2 = sb("w2", S, FC, D)
        b1, bg = (x_in[:, 8 * i:8 * i + 8, :, :].rearrange("p b i d -> p (b i d)")
                  .rearrange("p (g f) -> p g f", g=NG) for i in range(2))

        def carver(base):
            at = [0]

            def carve(*shape):
                a, b = at[0], at[0] + int(np.prod(shape))
                at[0] = b
                names = " ".join("abc"[:len(shape)])
                return base[:, a:b].rearrange(f"p ({names}) -> p {names}", **dict(zip("abc", shape)))
            return carve

        def part(name):
            a, b = SETUP_PARTS[name]
            return sw[:, a:b]

        def late(name):
            a, b = LATE_PARTS[name]
            return lw[:, a:b]

        def vec(name):
            a = SETUP_PARTS["vec"][0] + VEC[name]
            return sw[:, a:a + 1]

        ident = part("ident")
        conv_w = part("conv_w").rearrange("p (c k o) -> p c k o", c=IC, k=K)
        w_h = part("w_h").rearrange("p (c d) -> p c d", c=IC)
        w_gate = part("w_gate_t").rearrange("p (c d) -> p c d", c=IC)
        fc_t = part("fc_t").rearrange("p (c d) -> p c d", c=IC)
        out_t = part("out_t").rearrange("p (c d) -> p c d", c=IC)
        cproj = part("cproj").rearrange("p (c d) -> p c d", c=IC)
        wmod = part("wmod").rearrange("p (m d) -> p m d", m=6)
        mask_j = part("mask_j")
        mask_r = part("mask_r")

        c_tanh = sb("c_tanh", NS)
        c_silu = sb("c_silu", NS)
        mod = sb("mod", 6, NS)
        gate_sign = sb("gate_sign", 2, NS)
        gate_bias = sb("gate_bias", 2, NS)
        conv_m = sb("conv_m", IC, K, P)
        conv_bh = sb("conv_bh", IC)
        fc_g = sb("fc_g", IC, D)
        fc_c = sb("fc_c", IC, D)
        z_bias = sb("z_bias", 2)
        out_m = sb("out_m", D)
        slot_q = sb("slot_q", S)
        slot_bd = sb("slot_bd", H, S)
        key_q = sb("key_q", HC, P)
        key_b = sb("key_b", HC)
        slot_o = sb("slot_o", S)
        bias_o = sb("bias_o", 3)
        bq8 = sb("bq8", 1)
        means = sb("means", P)
        eps = sb("eps", TT)
        half_neg = sb("half_neg", TT)

        st1, mv1, ve1, rs1 = sb("st1", TT, 6), sb("mv1", TT, 2), sb("ve1", TT), sb("rs1", TT)
        sth, mvh, veh, rsh = sb("sth", TT, 6), sb("mvh", TT, 2), sb("veh", TT), sb("rsh", TT)
        st2, mv2, ve2, rs2 = sb("st2", TT, 6), sb("mv2", TT, 2), sb("ve2", TT), sb("rs2", TT)
        work = sb("work", 4096)
        carve = carver(work)
        n1 = carve(TT, D)
        hn_t = sb("hn_t", K - 1 + T)
        g_tanh = carve(IC, T)
        g_silu2 = carve(IC, T)
        h = carve(IC, T)
        y_s = carve(TT, D)
        z = carve(T)
        z_tanh = carve(T)
        z_silu2 = carve(T)
        out_g = carve(T)
        x1 = carve(T)
        n2 = carve(TT, D)
        h2_t = carve(T)
        q_t = sb("q_t", NS, T)
        val = sb("val", TT, D)
        mx = sb("mx", HC)
        mxb = sb("mxb", HC)
        ebias = sb("ebias", HC)
        prob = sb("prob", HC, T)
        prob_t = sb("prob_t", TT, HS)
        psum = sb("psum", HC)
        rsum = sb("rsum", HC)
        att_m = sb("att_m", HPC, S)
        att_t = sb("att_t", NS, S)
        o_t = sb("o_t", NS, S)
        st3, mv3, ve3, rs3 = sb("st3", 2, 6), sb("mv3", 2, 2), sb("ve3", 2), sb("rs3", 2)
        n3 = sb("n3", 2, D)
        ng3 = sb("ng3", NS, S)
        he_t = sb("he_t", S, Q)
        carve = carver(work)
        ub, gb_, us, gs = (carve(2, F) for _ in range(4))
        ug = conv_bd[:, :, :, :].rearrange("p c k o -> p c (k o)")
        ug_t = conv_m
        ye = sb("ye", 2, D)
        o2_t = sb("o2_t", NS, S)
        k2_t = sb("k2_t", NS, S)
        carve = carver(work)
        q_s = carve(T)
        k2_bd = carve(H, S)
        v2t_bd = carve(H, S)
        v2_t = carve(NS, S)
        v2w = carve(HC, D)
        e2 = carve(TT, HS)
        p2 = carve(TT, HS)
        y2g = carve(T)
        mx2 = sb("mx2", TT, H)
        sum2 = sb("sum2", TT, H)
        rsum2 = sb("rsum2", TT, H)
        s2_rows, p2_t = prob, prob_t

        ps = ctx.enter_context(nc.psum_tensor("ps", [P, 8, 512], F32))

        def bank(n, *shape):
            width = int(np.prod(shape))
            v = ps[:, n, 0:width]
            if len(shape) == 2:
                v = v.rearrange("p (a b) -> p a b", a=shape[0])
            return v

        gate_ps = bank(0, IC, T)
        conv_ps = (bank(1, T), ps[:, 5, T:2 * T])
        hT_ps = bank(2, TT, I)
        pT_ps = bank(3, TT, HS)
        s_ps = bank(3, HC, T)
        av_ps = ps[:, 4, T:T + P].rearrange("p (h s) -> p h s", s=S)
        y_ps = bank(4, TT, D)
        out_ps = bank(4, T)
        yT_ps = bank(5, T)
        hn_ps = bank(5, T)
        x1_ps = bank(6, TT, D)
        n2_ps = bank(6, T)
        q_ps = ps[:, 7, 0:T]
        v_ps = ps[:, 7, T:2 * T].rearrange("p (a b) -> p a b", a=TT)

        setup_in = [sem(f"setup_in{i}") for i in range(3)]
        x_in_sem = [sem(f"x_in{i}") for i in range(4)]
        xres_in = sem("xres_in")
        late_in = sem("late_in")
        expert_in = sem("expert_in")
        zeroed = sem("zeroed")
        conv_bd_ok = sem("conv_bd_ok")
        conv_m_ok = sem("conv_m_ok")
        mod_ok = sem("mod_ok")
        fc_c_ok = sem("fc_c_ok")
        (c_tanh_ok, c_ready, conv_m_mm, slot_q_mm, mod_mm, fc_g_ok, fc_mean_mm, slot_bd_ok, key_q_mm, out_m_mm,
         bias_mm, dve_chain) = (sem(n) for n in [
             "c_tanh_ok", "c_ready", "conv_m_mm", "slot_q_mm", "mod_mm", "fc_g_ok", "fc_mean_mm", "slot_bd_ok",
             "key_q_mm", "out_m_mm", "bias_mm", "dve_chain"])
        setup_done_dve = sem("setup_done_dve")
        setup_done_act = sem("setup_done_act")
        pool_ready = sem("pool_ready")
        ev = {n: sem(n) for n in [
            "st1_ok", "mv1_ok", "ve1_ok", "rs1_ok", "n1_ok", "hn_mm", "hn_ok", "gate_mm", "gtanh_ok", "gsilu_ok",
            "conv0_mm", "conv_mm", "h_ok", "hT_mm", "y_mm", "sth_ok", "mvh_ok", "veh_ok", "rsh_ok", "ys_ok", "yT_mm", "ztanh_ok",
            "zsilu_ok", "out_mm", "outg_ok", "x1_ok", "x1_kept", "x1_mm", "st2_ok", "mv2_ok", "ve2_ok", "rs2_ok", "n2_ok",
            "n2_mm", "h2_ok", "s_mm", "mx_ok", "mxb_ok", "ebias_ok", "exp_ok", "rsum_ok", "prob_ok", "qv_mm", "qv_ok", "pT_mm", "pT_ok",
            "av_mm", "attm_ok", "at_ok"]}
        o_mm, o_ok, oT_mm, e_chain, e_pool, eT_mm, he_ok = (sem(n) for n in [
            "o_mm", "o_ok", "oT_mm", "e_chain", "e_pool", "eT_mm", "he_ok"])
        u_mm, ub_ok, us_ok, ug_ok, ugT_mm, ugT_ok, ye_mm, ye_ok, yeT_mm, o2_ok, k2_mm, k2_ok = (sem(n) for n in [
            "u_mm", "ub_ok", "us_ok", "ug_ok", "ugT_mm", "ugT_ok", "ye_mm", "ye_ok", "yeT_mm", "o2_ok", "k2_mm",
            "k2_ok"])
        f = {n: sem("f_" + n) for n in [
            "k2bd_ok", "qs_ok", "v2bd_ok", "v2w_mm", "v2w_ok", "s2_mm", "mx2_ok", "s2_half", "s2_ok", "e2_half", "e2_ok", "sum2_ok", "rsum2_ok",
            "p2_half", "p2_ok", "p2T_mm", "p2T_ok", "y2_mm", "y2g_ok", "xo_ok"]}
        v2_mm, v2_ok = sem("v2_mm"), sem("v2_ok")
        stored = sem("stored")
        act_passed, dve_passed, pool_passed = sem("act_passed"), sem("dve_passed"), sem("pool_passed")

        block = ctx.enter_context(nc.Block())

        FIRST, LAST = -2, NS + 1
        LOOP = (2, NS - 2)
        LOOP2 = (3, NS - 1)
        LAST2 = NS + 1

        @block.sync
        def _(sp):
            def load_setup(i):
                c = slice(SETUP_LOADS[i], SETUP_LOADS[i + 1])
                sp.dma_start(sw[:, c], setup_w[:, c]).then_inc(setup_in[i], 16)

            def load_x(i):
                b = slice(X_LOADS[i], X_LOADS[i + 1])
                sp.dma_start(x_in[:, b, :, :], x_tok[:, b, :, :]).then_inc(x_in_sem[i], 16)

            load_setup(0)
            load_x(0)
            load_setup(1)
            load_setup(2)
            for i in range(1, 4):
                load_x(i)
            sp.dma_start(xres[:, :, :], x_feat).then_inc(xres_in, 16)
            sp.dma_start(lw[:, :], late_w).then_inc(late_in, 16)
            for e in range(0, S, 4):
                sp.dma_start(w1[:, e:e + 4, :], e_w1[:, e:e + 4, :]).then_inc(expert_in, 16)
                sp.dma_start(wg[:, e:e + 4, :], e_wg[:, e:e + 4, :]).then_inc(expert_in, 16)
                sp.dma_start(w2[:, e:e + 4, :, :], e_w2[:, e:e + 4, :, :]).then_inc(expert_in, 16)
            sp.wait_ge(ev["n1_ok"], NS)
            for src, dst in ((e_b1, b1), (e_bg, bg)):
                for j in range(EG):
                    sp.dma_start(dst[Q * j:Q * j + Q, :, :],
                                 src.rearrange("(g j) f -> j g f", j=EG)[j:j + 1].broadcast_to([Q, NG, F])
                                 ).then_inc(expert_in, 16)
            with sp.Fori(0, NS) as t:
                sp.wait_ge(f["xo_ok"], t + 1)
                sp.dma_start(out[:, bass.ds(t, 1), :], xres[:, bass.ds(t, 1), :]).then_inc(stored, 16)
            sp.wait_ge(stored, 16 * NS)
        EXPERT_LOADS = 16 * (2 * EG + 3 * (S // 4))

        @block.gpsimd
        def _(pool):
            nc.gpsimd.memset(conv_bd[:, :, :, :], 0.0).then_inc(zeroed, 1)
            nc.gpsimd.memset(eps[:, :], EPS)
            nc.gpsimd.memset(half_neg[:, :], -0.5)
            nc.gpsimd.memset(hn_t[:, 0:K - 1], 0.0)
            nc.gpsimd.memset(he_t[:, :, :], 0.0)
            nc.gpsimd.memset(means[:, :], 1.0 / I).then_inc(pool_ready, 1)

            def rsqrt(mv, ve, rs, mv_ok, ve_ok, rs_ok, b):
                wait(pool, mv_ok, b + 1)
                nc.gpsimd.tensor_tensor(ve[:, :], mv[:, :, 1], eps[:, :], ALU.add).then_inc(ve_ok, 1)
                wait(pool, ve_ok, b + 1)
                nc.gpsimd.tensor_tensor(rs[:, :], ve[:, :], half_neg[:, :], ALU.pow).then_inc(rs_ok, 1)

            def slot(t):
                if exists(t):
                    rsqrt(mvh, veh, rsh, ev["mvh_ok"], ev["veh_ok"], ev["rsh_ok"], t)
                if exists(t + 2):
                    rsqrt(mv1, ve1, rs1, ev["mv1_ok"], ev["ve1_ok"], ev["rs1_ok"], t + 2)
                if exists(t):
                    wait_alone(pool, ev["outg_ok"], t + 1, pool_passed)
                    xs = xres[:, bass.ds(t, 1), :].rearrange("p a t -> p (a t)")
                    nc.gpsimd.tensor_tensor(x1[:, :], xs, out_g[:, :], ALU.add).then_inc(ev["x1_ok"], 1)
                    wait_alone(pool, ev["x1_ok"], t + 1, pool_passed)
                    nc.gpsimd.tensor_copy(xs, x1[:, :]).then_inc(ev["x1_kept"], 1)
                if exists(t):
                    rsqrt(mv2, ve2, rs2, ev["mv2_ok"], ev["ve2_ok"], ev["rs2_ok"], t)

            pool.wait_ge(pool_ready, 1)
            for t in range(FIRST, 0):
                slot(t)
            pool.wait_ge(xres_in, 16)
            for t in range(0, LOOP[0]):
                slot(t)
            with pool.Fori(*LOOP) as t:
                slot(t)
            for t in range(LOOP[1], LAST + 1):
                slot(t)

            pool.wait_ge(e_chain, 2)
            nc.gpsimd.tensor_tensor(ve3[:, :], mv3[:, :, 1], eps[:, :], ALU.add).then_inc(e_pool, 1)
            pool.wait_ge(e_pool, 1)
            nc.gpsimd.tensor_tensor(rs3[:, :], ve3[:, :], half_neg[:, :], ALU.pow).then_inc(e_pool, 1)

            def keys(t):
                wait_alone(pool, f["s2_mm"], t, pool_passed)
                kb = k2_t[:, bass.ds(t, 1), :].broadcast_to([P, H, S])
                nc.gpsimd.tensor_tensor(k2_bd[:, :, :], kb, mask_j.unsqueeze(2).broadcast_to([P, H, S]),
                                        ALU.mult).then_inc(f["k2bd_ok"], 1)

            def values(t):
                wait_alone(pool, f["v2w_mm"], t, pool_passed)
                vb = v2_t[:, bass.ds(t, 1), :].broadcast_to([P, H, S])
                nc.gpsimd.tensor_tensor(v2t_bd[:, :, :], vb, mask_j.unsqueeze(2).broadcast_to([P, H, S]),
                                        ALU.mult).then_inc(f["v2bd_ok"], 1)

            def residual2(t):
                wait_alone(pool, f["y2g_ok"], t + 1, pool_passed)
                xs = xres[:, bass.ds(t, 1), :].rearrange("p a t -> p (a t)")
                nc.gpsimd.tensor_tensor(xs, xs, y2g[:, :], ALU.add).then_inc(f["xo_ok"], 1)

            def slot2(t):
                if exists(t + 1):
                    keys(t + 1)
                if exists(t):
                    values(t)
                if exists(t - 2):
                    residual2(t - 2)

            pool.wait_ge(k2_ok, 1)
            pool.wait_ge(v2_ok, 1)
            keys(0)
            for t in range(0, LOOP2[0]):
                slot2(t)
            with pool.Fori(*LOOP2) as t:
                slot2(t)
            for t in range(LOOP2[1], LAST2 + 1):
                slot2(t)

        @block.scalar
        def _(act):
            act.wait_ge(setup_in[0], 16)
            nc.scalar.activation(c_tanh[:, :], part("c_t"), ACT.Tanh, scale=0.5).then_inc(c_tanh_ok, 1)
            for c in range(IC):
                act.wait_ge(conv_m_mm, 1 + c)
                nc.scalar.mul(conv_m[:, c, :, :], bank(1 + c, K, P), 0.5).then_inc(conv_m_ok, 1)

            def modulated(dst, src, scale_at, shift_at, b):
                return nc.scalar.activation(dst, src, ACT.Identity, bias=mod[:, shift_at, bass.ds(b, 1)],
                                            scale=mod[:, scale_at, bass.ds(b, 1)])

            def slot(t):
                if exists(t + 1):
                    wait_alone(act, ev["hn_mm"], t + 2, act_passed)
                    modulated(hn_t[:, K - 1:K - 1 + T], hn_ps, 1, 0, t + 1).then_inc(ev["hn_ok"], 1)
                if exists(t + 1):
                    wait(act, ev["gate_mm"], t + 2)
                    nc.scalar.activation(g_tanh[:, :, :], gate_ps, ACT.Tanh, scale=0.5).then_inc(ev["gtanh_ok"], 1)
                if exists(t):
                    wait(act, ev["rsh_ok"], t + 1)
                    wait(act, ev["y_mm"], t + 1)
                    wait(act, ev["attm_ok"], t - 1)
                    wait(act, ev["yT_mm"], t)
                    for i in range(TT):
                        ins = nc.scalar.activation(y_s[:, i, :], y_ps[:, i, :], ACT.Identity, scale=rsh[:, i:i + 1])
                    ins.then_inc(ev["ys_ok"], 1)
                if exists(t - 1):
                    wait_alone(act, ev["n2_mm"], t, act_passed)
                    modulated(h2_t[:, :], n2_ps, 4, 3, t - 1).then_inc(ev["h2_ok"], 1)
                if exists(t):
                    if first(t):
                        act.wait_ge(setup_done_dve, 1)
                    wait(act, ev["yT_mm"], t + 1)
                    nc.scalar.activation(z[:, :], yT_ps, ACT.Identity, bias=z_bias[:, 0:1])
                    nc.scalar.activation(z_tanh[:, :], yT_ps, ACT.Tanh, bias=z_bias[:, 1:2],
                                         scale=0.5).then_inc(ev["ztanh_ok"], 1)
                if exists(t - 1):
                    wait(act, ev["ebias_ok"], t)
                    for c in range(HC):
                        ins = nc.scalar.activation(prob[:, c, :], s_ps[:, c, :], ACT.Exp, bias=ebias[:, c:c + 1],
                                                   accum_out=psum[:, c:c + 1])
                    ins.then_inc(ev["exp_ok"], 1)
                if exists(t):
                    wait_alone(act, ev["out_mm"], t + 1, act_passed)
                    nc.scalar.activation(out_g[:, :], out_ps, ACT.Identity, bias=gate_bias[:, 0, bass.ds(t, 1)],
                                         scale=mod[:, 2, bass.ds(t, 1)]).then_inc(ev["outg_ok"], 1)
                if exists(t - 1):
                    wait_alone(act, ev["qv_mm"], t, act_passed)
                    nc.scalar.copy(val[:, :, :], v_ps)
                    nc.scalar.activation(q_t[:, bass.ds(t - 1, 1), :].rearrange("p a t -> p (a t)"), q_ps, ACT.Identity,
                                         bias=bq8[:, :], scale=R8).then_inc(ev["qv_ok"], 1)
                if exists(t - 1):
                    wait(act, ev["pT_mm"], t)
                    nc.scalar.copy(prob_t[:, :, :], pT_ps).then_inc(ev["pT_ok"], 1)

            act.wait_ge(mod_ok, 1)
            for t in range(FIRST, 0):
                slot(t)
            act.wait_ge(key_q_mm, 1)
            nc.scalar.copy(key_q[:, :, :], bank(6, HC, P))
            act.wait_ge(out_m_mm, 1)
            nc.scalar.mul(out_m[:, :], bank(7, D), 0.5).then_inc(setup_done_act, 1)
            for t in range(0, LOOP[0]):
                slot(t)
            with act.Fori(*LOOP) as t:
                slot(t)
            for t in range(LOOP[1], LAST + 1):
                slot(t)

            def silus(g):
                act.wait_ge(ub_ok, 2 * g + 1)
                nc.scalar.activation(us[:, g % 2, :], ub[:, g % 2, :], ACT.Silu)
                act.wait_ge(ub_ok, 2 * g + 2)
                if g >= 2:
                    act.wait_ge(ug_ok, g - 1)
                nc.scalar.activation(gs[:, g % 2, :], gb_[:, g % 2, :], ACT.Silu).then_inc(us_ok, 1)

            def hidden_t(g):
                act.wait_ge(ugT_mm, g + 1)
                if g >= 2:
                    act.wait_ge(ye_mm, g - 1)
                nc.scalar.copy(ug_t[:, g % 2, :, :], bank(2, FC, P)).then_inc(ugT_ok, 1)

            def outputs(g):
                act.wait_ge(ye_mm, g + 1)
                nc.scalar.copy(ye[:, g % 2, :], bank(3, D)).then_inc(ye_ok, 1)

            for g in range(NG + 2):
                if g < NG:
                    silus(g)
                if 1 <= g < NG + 1:
                    hidden_t(g - 1)
                if g >= 2:
                    outputs(g - 2)

            halves2 = (("s2_half", "p2_half", "e2_half"), ("s2_ok", "p2_ok", "e2_ok"))

            def queries2(b):
                wait_alone(act, f["s2_mm"], b, act_passed)
                nc.scalar.copy(q_s[:, :], q_t[:, bass.ds(b, 1), :].rearrange("p a t -> p (a t)")
                               ).then_inc(f["qs_ok"], 1)

            def slot2(t):
                if exists(t - 2):
                    wait(act, f["p2T_mm"], t - 1)
                    nc.scalar.copy(p2_t[:, :, :], bank(1, HC, T)).then_inc(f["p2T_ok"], 1)
                if exists(t + 1):
                    queries2(t + 1)
                if exists(t):
                    for i in range(TT):
                        shifted, used, made = halves2[i]
                        wait(act, f[shifted], t + 1)
                        wait(act, f[used], t)
                        nc.scalar.activation(e2[:, i, :], s2_rows[:, i, :], ACT.Exp).then_inc(f[made], 1)
                if exists(t - 1):
                    wait(act, f["y2_mm"], t - 1)
                    wait(act, f["v2w_mm"], t)
                    nc.scalar.copy(v2w[:, :, :], bank(5, HC, D)).then_inc(f["v2w_ok"], 1)
                if exists(t - 2):
                    wait_alone(act, f["y2_mm"], t - 1, act_passed)
                    wait_alone(act, f["xo_ok"], t - 2, act_passed)
                    nc.scalar.activation(y2g[:, :], bank(4, T), ACT.Identity, bias=gate_bias[:, 1, bass.ds(t - 2, 1)],
                                         scale=mod[:, 5, bass.ds(t - 2, 1)]).then_inc(f["y2g_ok"], 1)

            queries2(0)
            for t in range(0, LOOP2[0]):
                slot2(t)
            with act.Fori(*LOOP2) as t:
                slot2(t)
            for t in range(LOOP2[1], LAST2 + 1):
                slot2(t)

        @block.tensor
        def _(pe):
            def mm(dst, lhs, rhs, first=True, last=True):
                return nc.tensor.matmul(dst, lhs, rhs, start=first, stop=last)

            def flip(dst, src):
                return nc.tensor.transpose(dst, src, ident)

            pe.wait_ge(conv_bd_ok, IC)
            for c in range(IC):
                mm(ps[:, 1 + c, :], w_h[:, c, :], conv_bd[:, c, :, :]).then_inc(conv_m_mm, 1)
            pe.wait_ge(c_ready, 1)
            pe.wait_ge(setup_in[1], 16)
            for m in range(6):
                ins = mm(ps[:, 0, m * NS:(m + 1) * NS], wmod[:, m, :], c_silu[:, :])
            ins.then_inc(mod_mm, 1)
            mm(bank(7, S), part("d_wq"), part("slot_t")).then_inc(slot_q_mm, 1)
            def norm_to_features(b):
                wait(pe, ev["n1_ok"], b + 1)
                wait(pe, ev["h_ok"], b)
                for i in range(TT):
                    ins = flip(hn_ps[:, i * P:(i + 1) * P], n1[:, i, :])
                ins.then_inc(ev["hn_mm"], 1)

            def gate(b):
                wait(pe, ev["hn_ok"], b + 1)
                wait(pe, ev["gsilu_ok"], b)
                for c in range(IC):
                    ins = mm(gate_ps[:, c, :], w_gate[:, c, :], hn_t[:, K - 1:K - 1 + T])
                ins.then_inc(ev["gate_mm"], 1)

            def conv(b, c, taps):
                if c == 0 and taps[0] == 0:
                    wait(pe, ev["h_ok"], b)
                for k in taps:
                    ins = mm(conv_ps[c], conv_m[:, c, k, :], hn_t[:, k:k + T], k == 0, k == K - 1)
                if taps[-1] == K - 1:
                    ins.then_inc(ev["conv_mm"] if c == IC - 1 else ev["conv0_mm"], 1)

            def inner_to_tokens(b):
                wait(pe, ev["h_ok"], b + 1)
                wait(pe, ev["sth_ok"], b)
                for i in range(TT):
                    for c in range(IC):
                        ins = flip(hT_ps[:, i, c * P:(c + 1) * P], h[:, c, i * P:(i + 1) * P])
                ins.then_inc(ev["hT_mm"], 1)

            def inner_product(b):
                wait(pe, ev["outg_ok"], b)
                for i in range(TT):
                    for c in range(IC):
                        ins = mm(y_ps[:, i, :], h[:, c, i * P:(i + 1) * P], fc_c[:, c, :], c == 0, c == IC - 1)
                ins.then_inc(ev["y_mm"], 1)

            def inner_to_features(b):
                wait(pe, ev["ys_ok"], b + 1)
                wait(pe, ev["hn_ok"], b + 2)
                for i in range(TT):
                    ins = flip(yT_ps[:, i * P:(i + 1) * P], y_s[:, i, :])
                ins.then_inc(ev["yT_mm"], 1)

            def project_out(b):
                if first(b):
                    pe.wait_ge(setup_done_act, 1)
                wait(pe, ev["zsilu_ok"], b + 1)
                for c in range(IC):
                    mm(out_ps, out_t[:, c, :], h[:, c, :], c == 0, False)
                mm(out_ps, out_m[:, :], z_silu2[:, :], False, True).then_inc(ev["out_mm"], 1)

            def residual_to_tokens(b):
                wait(pe, ev["x1_ok"], b + 1)
                wait(pe, ev["h2_ok"], b)
                for i in range(TT):
                    ins = flip(x1_ps[:, i, :], x1[:, i * P:(i + 1) * P])
                ins.then_inc(ev["x1_mm"], 1)

            def norm2_to_features(b):
                wait(pe, ev["n2_ok"], b + 1)
                for i in range(TT):
                    ins = flip(n2_ps[:, i * P:(i + 1) * P], n2[:, i, :])
                ins.then_inc(ev["n2_mm"], 1)

            def scores(b):
                wait(pe, ev["h2_ok"], b + 1)
                wait(pe, ev["pT_ok"], b)
                for c in range(HC):
                    ins = mm(s_ps[:, c, :], key_q[:, c, :], h2_t[:, :])
                ins.then_inc(ev["s_mm"], 1)

            def queries_values(b):
                wait(pe, ev["qv_ok"], b)
                mm(q_ps, part("c_wq"), h2_t[:, :])
                for i in range(TT):
                    ins = mm(v_ps[:, i, :], h2_t[:, i * P:(i + 1) * P], part("d_wv"))
                ins.then_inc(ev["qv_mm"], 1)

            def prob_to_tokens(b):
                wait(pe, ev["prob_ok"], b + 1)
                for i in range(TT):
                    for c in range(HC):
                        ins = flip(pT_ps[:, i, c * P:(c + 1) * P], prob[:, c, i * P:(i + 1) * P])
                ins.then_inc(ev["pT_mm"], 1)

            def attend(b):
                wait(pe, ev["pT_ok"], b + 1)
                wait(pe, ev["qv_ok"], b + 1)
                wait(pe, ev["outg_ok"], b + 2)
                for i in range(TT):
                    for c in range(HC):
                        j = slice(c * JC, (c + 1) * JC)
                        ins = mm(av_ps[j], val[:, i, j], prob_t[:, i, c * P:(c + 1) * P], i == 0, i == TT - 1)
                ins.then_inc(ev["av_mm"], 1)

            def slot(t):
                if exists(t + 1):
                    norm_to_features(t + 1)
                if exists(t):
                    inner_to_tokens(t)
                if exists(t):
                    inner_product(t)
                if exists(t - 2):
                    attend(t - 2)
                if exists(t + 1):
                    gate(t + 1)
                if exists(t + 1):
                    conv(t + 1, 0, range(0, K // 2))
                if exists(t - 1):
                    norm2_to_features(t - 1)
                if exists(t + 1):
                    conv(t + 1, 0, range(K // 2, K))
                if exists(t):
                    inner_to_features(t)
                if exists(t - 1):
                    scores(t - 1)
                if exists(t - 1):
                    queries_values(t - 1)
                if exists(t):
                    project_out(t)
                if exists(t + 1):
                    conv(t + 1, 1, range(0, K // 2))
                if exists(t + 1):
                    conv(t + 1, 1, range(K // 2, K))
                if exists(t):
                    residual_to_tokens(t)
                if exists(t - 1):
                    prob_to_tokens(t - 1)

            pe.wait_ge(conv_m_ok, IC)
            for t in range(FIRST, 0):
                slot(t)
            pe.wait_ge(setup_in[2], 16)
            pe.wait_ge(fc_g_ok, 1)
            pe.wait_ge(pool_ready, 1)
            for c in range(IC):
                ins = mm(bank(3, D), means[:, :], fc_g[:, c, :], c == 0, c == IC - 1)
            ins.then_inc(fc_mean_mm, 1)
            pe.wait_ge(slot_bd_ok, 1)
            mm(bank(6, HS), part("d_wk_t"), slot_bd[:, :, :]).then_inc(key_q_mm, 1)
            for c in range(IC):
                ins = mm(bank(7, D), cproj[:, c, :], out_t[:, c, :], c == 0, c == IC - 1)
            ins.then_inc(out_m_mm, 1)
            pe.wait_ge(fc_c_ok, 1)
            for c in range(IC):
                mm(ps[:, 3, 0:1], fc_t[:, c, :], vec(f"ln_b{c}"), c == 0, c == IC - 1)
            for c in range(IC):
                mm(ps[:, 3, 1:2], out_t[:, c, :], vec(f"cproj_b{c}"), c == 0, c == IC - 1)
            for c in range(HC):
                mm(ps[:, 3, 2 + c:3 + c], slot_bd[:, c * HPC:(c + 1) * HPC, :], vec("d_bk"))
            mm(ps[:, 3, 4:5], part("d_wo"), vec("d_bv"))
            mm(ps[:, 3, 5:6], part("c_wo"), vec("c_bv")).then_inc(bias_mm, 1)
            for t in range(0, LOOP[0]):
                slot(t)
            with pe.Fori(*LOOP) as t:
                slot(t)
            for t in range(LOOP[1], LAST + 1):
                slot(t)

            pe.wait_ge(ev["at_ok"], NS)
            pe.wait_ge(late_in, 16)
            pe.wait_ge(expert_in, EXPERT_LOADS)
            mm(bank(0, NS * S), part("d_wo"), att_t[:, :, :]).then_inc(o_mm, 1)
            pe.wait_ge(o_ok, 1)
            for i in range(2):
                ins = flip(ps[:, 1, i * P:(i + 1) * P], o_t[:, i * NS // 2:(i + 1) * NS // 2, :])
            ins.then_inc(oT_mm, 1)
            pe.wait_ge(e_chain, 3)
            for i in range(2):
                ins = flip(ps[:, 2, i * P:(i + 1) * P], n3[:, i, :])
            ins.then_inc(eT_mm, 1)
            pe.wait_ge(he_ok, 1)

            def hidden(g):
                for n, w in ((4, w1), (6, wg)):
                    if g >= 2:
                        pe.wait_ge(ub_ok, 2 * (g - 2) + (1 if n == 4 else 2))
                    for j in range(EG):
                        ins = mm(ps[Q * j:Q * j + Q, n + g % 2, :], he_t[:, EG * g + j, :], w[:, EG * g + j, :])
                    ins.then_inc(u_mm, 1)

            def hidden_to_rows(g):
                pe.wait_ge(ug_ok, g + 1)
                if g >= 1:
                    pe.wait_ge(ugT_ok, g)
                for k in range(FC):
                    ins = flip(ps[:, 2, k * P:(k + 1) * P], ug[:, g % 2, k * P:(k + 1) * P])
                ins.then_inc(ugT_mm, 1)

            def hidden_product(g):
                pe.wait_ge(ugT_ok, g + 1)
                if g >= 1:
                    pe.wait_ge(ye_ok, g)
                for k in range(FC):
                    for j in range(EG):
                        ins = mm(ps[Q * j:Q * j + Q, 3, 0:D], ug_t[:, g % 2, k, Q * j:Q * j + Q],
                                 w2[:, EG * g + j, k, :], k == 0, k == FC - 1)
                ins.then_inc(ye_mm, 1)

            def to_slots(g):
                pe.wait_ge(ye_ok, g + 1)
                if g >= 2:
                    pe.wait_ge(o2_ok, g - 1)
                flip(ps[:, g % 2, 0:P], ye[:, g % 2, :]).then_inc(yeT_mm, 1)

            for g in range(NG + 3):
                if g < NG:
                    hidden(g)
                if 2 <= g < NG + 2:
                    hidden_product(g - 2)
                if 1 <= g < NG + 1:
                    hidden_to_rows(g - 1)
                if 3 <= g < NG + 3:
                    to_slots(g - 3)
            pe.wait_ge(o2_ok, NG)
            mm(bank(4, NS * S), late("c_wk"), o2_t[:, :, :]).then_inc(k2_mm, 1)
            mm(bank(5, NS * S), late("c_wv"), o2_t[:, :, :]).then_inc(v2_mm, 1)
            pe.wait_ge(v2_ok, 1)

            def scores2(b):
                wait(pe, f["k2bd_ok"], b + 1)
                wait(pe, f["qs_ok"], b + 1)
                wait(pe, f["s2_ok"], b)
                for i in range(TT):
                    ins = mm(ps[:, 0, i * HS:(i + 1) * HS], q_s[:, i * P:(i + 1) * P], k2_bd[:, :, :])
                ins.then_inc(f["s2_mm"], 1)

            def probs2_to_rows(b):
                wait(pe, f["p2_ok"], b + 1)
                wait(pe, f["p2T_ok"], b)
                for c in range(HC):
                    for i in range(TT):
                        ins = flip(ps[:, 1, c * T + i * P:c * T + (i + 1) * P], p2[:, i, c * P:(c + 1) * P])
                ins.then_inc(f["p2T_mm"], 1)

            def values2(b):
                wait(pe, f["v2bd_ok"], b + 1)
                wait(pe, f["v2w_ok"], b)
                for c in range(HC):
                    ins = mm(ps[:, 5, c * D:(c + 1) * D], v2t_bd[:, c * HPC:(c + 1) * HPC, :], part("c_wo"))
                ins.then_inc(f["v2w_mm"], 1)

            def outputs2(b):
                wait(pe, f["p2T_ok"], b + 1)
                wait(pe, f["v2w_ok"], b + 1)
                wait(pe, f["y2g_ok"], b)
                for c in range(HC):
                    ins = mm(bank(4, T), v2w[:, c, :], p2_t[:, c, :], c == 0, c == HC - 1)
                ins.then_inc(f["y2_mm"], 1)

            def slot2(t):
                if exists(t):
                    scores2(t)
                if exists(t - 2):
                    probs2_to_rows(t - 2)
                if exists(t - 1):
                    values2(t - 1)
                if exists(t - 2):
                    outputs2(t - 2)

            for t in range(0, LOOP2[0]):
                slot2(t)
            with pe.Fori(*LOOP2) as t:
                slot2(t)
            for t in range(LOOP2[1], LAST2 + 1):
                slot2(t)

        @block.vector
        def _(dve):
            v = nc.vector
            links = [0]

            def chain(ins):
                links[0] += 1
                ins.then_inc(dve_chain, 1)
                dve.wait_ge(dve_chain, links[0])

            def over_samples(x):
                return x.unsqueeze(1).broadcast_to([P, NS, S])

            dve.wait_ge(setup_in[0], 16)
            dve.wait_ge(zeroed, 1)
            for c in range(IC):
                for q in range(P // CG):
                    r = slice(q * CG, (q + 1) * CG)
                    ins = v.tensor_copy(conv_bd[r, c, :, r], conv_w[r, c, :, :])
                ins.then_inc(conv_bd_ok, 1)
            dve.wait_ge(c_tanh_ok, 1)
            chain(v.scalar_tensor_tensor(out=c_silu[:, :], in0=c_tanh[:, :], scalar=1.0, in1=part("c_t"),
                                         op0=ALU.add, op1=ALU.mult))
            v.tensor_scalar(c_silu[:, :], c_silu[:, :], 0.5, None, ALU.mult).then_inc(c_ready, 1)

            def more_setup():
                dve.wait_ge(mod_mm, 1)
                chain(v.tensor_copy(mod[:, :, :], bank(0, 6, NS)))
                for m in (1, 4):
                    ins = v.tensor_scalar(mod[:, m, :], mod[:, m, :], 1.0, None, ALU.add)
                ins.then_inc(mod_ok, 1)
                dve.wait_ge(slot_q_mm, 1)
                chain(v.tensor_scalar(slot_q[:, :], bank(7, S), vec("d_bq"), R8, ALU.add, ALU.mult))
                v.tensor_tensor(slot_bd[:, :, :], mask_j.unsqueeze(2).broadcast_to([P, H, S]),
                                slot_q[:, :].unsqueeze(1).broadcast_to([P, H, S]), ALU.mult).then_inc(slot_bd_ok, 1)
                v.tensor_scalar(bq8[:, :], vec("c_bq"), R8, None, ALU.mult)
                for c in range(IC):
                    v.tensor_scalar(conv_bh[:, c:c + 1], vec(f"conv_b{c}"), 0.5, None, ALU.mult)
                for m, n in ((2, 0), (5, 1)):
                    gate_m, sign = mod[:, m, :], gate_sign[:, n, :]
                    chain(v.tensor_scalar(sign, gate_m, -1.0, None, ALU.mult))
                    chain(v.tensor_tensor(gate_bias[:, n, :], sign, gate_m, ALU.max))
                    chain(v.tensor_scalar(sign, gate_m, 0.0, 2.0, ALU.is_ge, ALU.mult))
                    chain(v.tensor_scalar(sign, sign, -1.0, None, ALU.add))
                    chain(v.scalar_tensor_tensor(out=gate_m, in0=gate_bias[:, n, :], scalar=0.25, in1=sign,
                                                 op0=ALU.max, op1=ALU.mult))
                dve.wait_ge(setup_in[2], 16)
                for c in range(IC):
                    ins = v.tensor_scalar(fc_g[:, c, :], fc_t[:, c, :], vec(f"ln_g{c}"), None, ALU.mult)
                ins.then_inc(fc_g_ok, 1)

            def finish_setup():
                dve.wait_ge(fc_mean_mm, 1)
                for c in range(IC):
                    ins = v.tensor_tensor(fc_c[:, c, :], fc_g[:, c, :], bank(3, D), ALU.subtract)
                ins.then_inc(fc_c_ok, 1)
                dve.wait_ge(bias_mm, 1)
                chain(v.tensor_tensor(z_bias[:, 0:1], ps[:, 3, 0:1], vec("fc_b"), ALU.add))
                v.tensor_scalar(z_bias[:, 1:2], z_bias[:, 0:1], 0.5, None, ALU.mult)
                v.tensor_copy(bias_o[:, 0:1], ps[:, 3, 1:2])
                v.tensor_copy(key_b[:, :], ps[:, 3, 2:4])
                v.tensor_tensor(bias_o[:, 1:2], ps[:, 3, 4:5], vec("d_bo"), ALU.add)
                chain(v.tensor_tensor(bias_o[:, 2:3], ps[:, 3, 5:6], vec("c_bo"), ALU.add))
                v.tensor_scalar(slot_o[:, :], part("slot_t"), bias_o[:, 1:2], None, ALU.add)
                v.tensor_scalar(gate_bias[:, 0, :], mod[:, 2, :], bias_o[:, 0:1], None, ALU.mult)
                v.tensor_scalar(gate_bias[:, 1, :], mod[:, 5, :], bias_o[:, 2:3], None,
                                ALU.mult).then_inc(setup_done_dve, 1)

            def stats(st, mv, srcs, st_ok, mv_ok, b):
                for i in range(TT):
                    ins = v.bn_stats(st[:, i, :], srcs[i])
                ins.then_inc(st_ok, 1)
                wait_alone(dve, st_ok, b + 1, dve_passed)
                for i in range(TT):
                    ins = v.bn_aggr(mv[:, i, :], st[:, i, :])
                ins.then_inc(mv_ok, 1)

            def x_tile(b, i):
                return x_in[:, bass.ds(b, 1), i, :].rearrange("p a d -> p (a d)")

            def convolved(c):
                return v.scalar_tensor_tensor(out=h[:, c, :], in0=conv_ps[c], scalar=conv_bh[:, c:c + 1],
                                              in1=g_silu2[:, c, :], op0=ALU.add, op1=ALU.mult)

            def slot(t):
                if exists(t):
                    wait(dve, ev["hT_mm"], t + 1)
                    stats(sth, mvh, [hT_ps[:, i, :] for i in range(TT)], ev["sth_ok"], ev["mvh_ok"], t)
                if exists(t - 1):
                    wait(dve, ev["rs2_ok"], t)
                    for i in range(TT):
                        ins = v.tensor_scalar(n2[:, i, :], x1_ps[:, i, :], mv2[:, i, 0:1], rs2[:, i:i + 1],
                                              ALU.subtract, ALU.mult)
                    ins.then_inc(ev["n2_ok"], 1)
                if exists(t - 2):
                    wait(dve, ev["av_mm"], t - 1)
                    v.tensor_tensor(att_m[:, :, :], av_ps, mask_r.unsqueeze(2).broadcast_to([P, HPC, S]),
                                    ALU.mult).then_inc(ev["attm_ok"], 1)
                    wait(dve, ev["attm_ok"], t - 1)
                    v.tensor_reduce(att_t[:, bass.ds(t - 2, 1), :].rearrange("p a s -> p (a s)"),
                                    att_m[:, :, :].rearrange("p h s -> p s h"), AX_X, ALU.add).then_inc(ev["at_ok"], 1)
                if exists(t + 2):
                    stats(st1, mv1, [x_tile(t + 2, i) for i in range(TT)], ev["st1_ok"], ev["mv1_ok"], t + 2)
                if exists(t + 1):
                    wait(dve, ev["gtanh_ok"], t + 2)
                    v.scalar_tensor_tensor(out=g_silu2[:, :, :], in0=g_tanh[:, :, :], scalar=1.0, in1=gate_ps,
                                           op0=ALU.add, op1=ALU.mult).then_inc(ev["gsilu_ok"], 1)
                if exists(t):
                    wait(dve, ev["ztanh_ok"], t + 1)
                    v.scalar_tensor_tensor(out=z_silu2[:, :], in0=z_tanh[:, :], scalar=1.0, in1=z[:, :],
                                           op0=ALU.add, op1=ALU.mult).then_inc(ev["zsilu_ok"], 1)
                if exists(t - 1):
                    wait(dve, ev["s_mm"], t)
                    v.tensor_reduce(mx[:, :], s_ps, AX_X, ALU.max).then_inc(ev["mx_ok"], 1)
                    wait(dve, ev["mx_ok"], t)
                    v.tensor_tensor(mxb[:, :], mx[:, :], key_b[:, :], ALU.add).then_inc(ev["mxb_ok"], 1)
                    wait(dve, ev["mxb_ok"], t)
                    v.tensor_tensor(ebias[:, :], key_b[:, :], mxb[:, :], ALU.subtract).then_inc(ev["ebias_ok"], 1)
                if exists(t + 2):
                    wait(dve, ev["rs1_ok"], t + 3)
                    wait(dve, ev["hn_mm"], t + 2)
                    for i in range(TT):
                        ins = v.tensor_scalar(n1[:, i, :], x_tile(t + 2, i), mv1[:, i, 0:1], rs1[:, i:i + 1],
                                              ALU.subtract, ALU.mult)
                    ins.then_inc(ev["n1_ok"], 1)
                if exists(t + 1):
                    wait(dve, ev["gsilu_ok"], t + 2)
                    wait(dve, ev["conv0_mm"], t + 2)
                    wait(dve, ev["out_mm"], t + 1)
                    convolved(0)
                if exists(t - 1):
                    wait(dve, ev["exp_ok"], t)
                    v.reciprocal(rsum[:, :], psum[:, :]).then_inc(ev["rsum_ok"], 1)
                    wait(dve, ev["rsum_ok"], t)
                    for c in range(HC):
                        ins = v.tensor_scalar(prob[:, c, :], prob[:, c, :], rsum[:, c:c + 1], None, ALU.mult)
                    ins.then_inc(ev["prob_ok"], 1)
                if exists(t + 1):
                    wait(dve, ev["conv_mm"], t + 2)
                    convolved(1).then_inc(ev["h_ok"], 1)
                if exists(t):
                    wait(dve, ev["x1_mm"], t + 1)
                    stats(st2, mv2, [x1_ps[:, i, :] for i in range(TT)], ev["st2_ok"], ev["mv2_ok"], t)

            dve.wait_ge(x_in_sem[0], 16)
            slot(FIRST)
            more_setup()
            slot(FIRST + 1)
            finish_setup()
            dve.wait_ge(x_in_sem[1], 16)
            for t in range(FIRST + 2, LOOP[0]):
                slot(t)
            for s_ in x_in_sem[2:]:
                dve.wait_ge(s_, 16)
            with dve.Fori(*LOOP) as t:
                slot(t)
            for t in range(LOOP[1], LAST + 1):
                slot(t)

            dve.wait_ge(late_in, 16)
            dve.wait_ge(o_mm, 1)
            v.tensor_tensor(o_t[:, :, :], bank(0, NS, S), over_samples(slot_o[:, :]), ALU.add).then_inc(o_ok, 1)
            dve.wait_ge(oT_mm, 1)
            for i in range(2):
                ins = v.bn_stats(st3[:, i, :], ps[:, 1, i * P:(i + 1) * P])
            ins.then_inc(e_chain, 1)
            dve.wait_ge(e_chain, 1)
            for i in range(2):
                ins = v.bn_aggr(mv3[:, i, :], st3[:, i, :])
            ins.then_inc(e_chain, 1)
            dve.wait_ge(e_pool, 2)
            for i in range(2):
                ins = v.tensor_scalar(n3[:, i, :], ps[:, 1, i * P:(i + 1) * P], mv3[:, i, 0:1], rs3[:, i:i + 1],
                                      ALU.subtract, ALU.mult)
            ins.then_inc(e_chain, 1)
            v.tensor_tensor(o_t[:, :, :], o_t[:, :, :], over_samples(late("e_b2_t")), ALU.add)
            dve.wait_ge(eT_mm, 1)
            chain(v.tensor_tensor(ng3[:, :, :], bank(2, NS, S), over_samples(late("e_g_t")), ALU.mult))
            v.tensor_tensor(he_t[:, :, 0:NS].rearrange("p s b -> p b s"), ng3[:, :, :], over_samples(late("e_b_t")),
                            ALU.add).then_inc(he_ok, 1)
            dve.wait_ge(expert_in, EXPERT_LOADS)

            def hidden_biases(g):
                for n, (b, dst) in enumerate(((b1, ub), (bg, gb_))):
                    dve.wait_ge(u_mm, 2 * g + n + 1)
                    if g >= 2:
                        dve.wait_ge(us_ok, g - 1)
                    v.tensor_tensor(dst[:, g % 2, :], ps[:, 4 + 2 * n + g % 2, :], b[:, g, :],
                                    ALU.add).then_inc(ub_ok, 1)

            def gated(g):
                dve.wait_ge(us_ok, g + 1)
                if g >= 2:
                    dve.wait_ge(ugT_mm, g - 1)
                v.tensor_tensor(ug[:, g % 2, :], us[:, g % 2, :], gs[:, g % 2, :], ALU.mult).then_inc(ug_ok, 1)

            def add_to_slots(g):
                dve.wait_ge(yeT_mm, g + 1)
                e = slice(EG * g, EG * (g + 1))
                y = ps[:, g % 2, 0:P].rearrange("p (j q) -> p q j", j=EG)[:, 0:NS, :]
                v.tensor_tensor(o2_t[:, :, e], o_t[:, :, e], y, ALU.add).then_inc(o2_ok, 1)

            for g in range(NG + 3):
                if g < NG:
                    hidden_biases(g)
                if 1 <= g < NG + 1:
                    gated(g - 1)
                if g >= 3:
                    add_to_slots(g - 3)
            dve.wait_ge(k2_mm, 1)
            v.tensor_scalar(k2_t[:, :, :], bank(4, NS, S), vec("c_bk"), None, ALU.add).then_inc(k2_ok, 1)

            dve.wait_ge(v2_mm, 1)
            v.tensor_copy(v2_t[:, :, :], bank(5, NS, S)).then_inc(v2_ok, 1)

            def by_head(x):
                return x.rearrange("p (h s) -> p h s", s=S)

            def slot2(t):
                if exists(t - 1):
                    for i, half in enumerate(("e2_half", "e2_ok")):
                        wait(dve, f[half], t)
                        ins = v.tensor_reduce(sum2[:, i, :], by_head(e2[:, i, :]), AX_X, ALU.add)
                    ins.then_inc(f["sum2_ok"], 1)
                if exists(t):
                    wait(dve, f["s2_mm"], t + 1)
                    v.tensor_reduce(mx2[:, :, :], ps[:, 0, :].rearrange("p (a s) -> p a s", s=S), AX_X,
                                    ALU.max).then_inc(f["mx2_ok"], 1)
                if exists(t - 1):
                    wait(dve, f["sum2_ok"], t)
                    v.reciprocal(rsum2[:, :, :], sum2[:, :, :]).then_inc(f["rsum2_ok"], 1)
                if exists(t):
                    wait(dve, f["mx2_ok"], t + 1)
                    for i, half in enumerate(("s2_half", "s2_ok")):
                        v.tensor_tensor(by_head(s2_rows[:, i, :]), by_head(ps[:, 0, i * HS:(i + 1) * HS]),
                                        mx2[:, i, :].unsqueeze(2).broadcast_to([P, H, S]),
                                        ALU.subtract).then_inc(f[half], 1)
                if exists(t - 1):
                    wait(dve, f["p2T_mm"], t - 1)
                    wait(dve, f["rsum2_ok"], t)
                    for i, half in enumerate(("p2_half", "p2_ok")):
                        v.tensor_tensor(by_head(p2[:, i, :]), by_head(e2[:, i, :]),
                                        rsum2[:, i, :].unsqueeze(2).broadcast_to([P, H, S]),
                                        ALU.mult).then_inc(f[half], 1)

            for t in range(0, LOOP2[0]):
                slot2(t)
            with dve.Fori(*LOOP2) as t:
                slot2(t)
            for t in range(LOOP2[1], LAST2 + 1):
                slot2(t)


def kernel(**inputs):
    import concourse.bacc as bacc
    from concourse.bass_utils import run_bass_kernel_spmd

    a = {k: np.asarray(v) for k, v in inputs.items()}

    def attn(name):
        return a["L0_attn_" + name]

    def ffn(name):
        return a["L0_ffn_" + name]

    def by_rows(w):
        return w.reshape(-1, P, w.shape[-1]).transpose(1, 0, 2).reshape(P, -1)

    feature = np.arange(D)
    mask_j = (feature[:, None] // DH == np.arange(H)).astype(np.float32)
    mask_r = (feature[:, None] % JC // DH == np.arange(HPC)).astype(np.float32)

    x = attn("hidden_states")
    w_in = attn("in_proj_w")
    vecs = {
        "conv_b": attn("conv_b"), "ln_g": attn("ln_g"), "ln_b": attn("ln_b"), "cproj_b": attn("cproj_b"),
        "fc_b": attn("fc_b"), "d_bq": ffn("d_bq"), "d_bk": ffn("d_bk"), "d_bv": ffn("d_bv"), "d_bo": ffn("d_bo"),
        "c_bq": ffn("c_bq"), "c_bk": ffn("c_bk"), "c_bv": ffn("c_bv"), "c_bo": ffn("c_bo")}
    vec = np.stack([vecs[n] if n in vecs else vecs[n[:-1]][int(n[-1]) * P:(int(n[-1]) + 1) * P] for n in VEC], 1)
    setup = {
        "ident": np.eye(P, dtype=np.float32), "c_t": a["L0_c"].T, "slot_t": ffn("slot_query")[0].T, "vec": vec,
        "pad": np.zeros((P, 3), np.float32), "wmod": a["L0_wmod"], "w_h": by_rows(w_in[:I]), "w_gate_t": w_in[I:].T,
        "fc_t": by_rows(attn("fc_w").T), "out_t": by_rows(attn("out_w").T), "cproj": by_rows(attn("cproj_w")),
        "conv_w": attn("conv_w").reshape(IC, G // IC, CG, CG, K).transpose(1, 3, 0, 4, 2).reshape(P, -1),
        "d_wq": ffn("d_Wq"), "d_wk_t": ffn("d_Wk").T, "d_wv": ffn("d_Wv"), "d_wo": ffn("d_Wo"),
        "c_wq": ffn("c_Wq"), "c_wo": ffn("c_Wo"), "mask_j": mask_j, "mask_r": mask_r}
    late = {
        "c_wk": ffn("c_Wk"), "c_wv": ffn("c_Wv"), "e_g_t": ffn("e_ln_g").T, "e_b_t": ffn("e_ln_b").T,
        "e_b2_t": ffn("e_b2").T}
    arrays = {
        "x_tok": x.reshape(NS, TT, P, D).transpose(2, 0, 1, 3),
        "x_feat": x.transpose(2, 0, 1),
        "setup_w": np.concatenate([setup[n] for n in SETUP_PARTS], 1),
        "late_w": np.concatenate([late[n] for n in LATE_PARTS], 1),
        "e_w1": ffn("e_W1").transpose(1, 0, 2),
        "e_wg": ffn("e_Wg").transpose(1, 0, 2),
        "e_w2": ffn("e_W2").reshape(S, FC, P, D).transpose(2, 0, 1, 3),
        "e_b1": ffn("e_b1"),
        "e_bg": ffn("e_bg"),
    }
    arrays = {k: np.ascontiguousarray(v) for k, v in arrays.items()}
    nc = bacc.Bacc("TRN2", target_bir_lowering=False, num_devices=1)
    args = {k: nc.dram_tensor(k, v.shape, F32, kind="ExternalInput").ap() for k, v in arrays.items()}
    out = nc.dram_tensor("out", (P, NS, T), F32, kind="ExternalOutput").ap()
    adaln_block_kernel(nc, **args, out=out)
    r = run_bass_kernel_spmd(nc, [arrays], core_ids=[0])
    return np.ascontiguousarray(r.results[0]["out"].transpose(1, 2, 0))
```

```python
from contextlib import ExitStack

import numpy as np

import concourse.bass as bass
from concourse import mybir

F32 = mybir.dt.float32
F32R = mybir.dt.float32r
ALU = mybir.AluOpType
ACT = mybir.ActivationFunctionType
AX_X = mybir.AxisListType.X

P = 128
D = 128
NS = 16
T = 256
TT = T // P
I = 256
IC = I // P
K = 4
CG = 32
G = I // CG
H = 16
DH = D // H
S = 16
HS = H * S
HC = HS // P
HPC = H // HC
F = 512
FC = F // P
Q = 32
EG = P // Q
NG = S // EG
JC = D // HC
EPS = 1e-5
R8 = float(1.0 / np.sqrt(DH))


def columns(parts):
    at, out = 0, {}
    for name, width in parts:
        out[name] = (at, at + width)
        at += width
    return out, at


SETUP_PARTS, SETUP_W = columns([
    ("ident", P), ("c_t", NS), ("slot_t", S), ("vec", 17), ("pad", 3), ("w_h", IC * D), ("conv_w", IC * K * CG),
    ("wmod", 6 * D), ("d_wq", D), ("w_gate_t", I), ("mask_j", H), ("mask_r", HPC),
    ("fc_t", IC * D), ("out_t", IC * D), ("cproj", IC * D), ("d_wk_t", D), ("d_wv", D), ("d_wo", D), ("c_wq", D),
    ("c_wo", D)])
SETUP_LOADS = (0, SETUP_PARTS["wmod"][0], SETUP_PARTS["fc_t"][0], SETUP_W)
X_LOADS = (0, 2, 4, 10, NS)
LATE_PARTS, LATE_W = columns([
    ("c_wk", D), ("c_wv", D), ("e_g_t", S), ("e_b_t", S), ("e_b2_t", S)])
VEC = {n: i for i, n in enumerate([
    "conv_b0", "conv_b1", "ln_g0", "ln_g1", "ln_b0", "ln_b1", "cproj_b0", "cproj_b1", "fc_b",
    "d_bq", "d_bk", "d_bv", "d_bo", "c_bq", "c_bk", "c_bv", "c_bo"])}


def exists(b):
    return not isinstance(b, int) or 0 <= b < NS


def first(b):
    return isinstance(b, int) and b == 0


def wait(eng, sem, count):
    if isinstance(count, int):
        count = min(count, NS)
        if count <= 0:
            return
    eng.wait_ge(sem, count)


def wait_alone(eng, sem, count, passed):
    wait(eng, sem, count)
    if not isinstance(count, int):
        eng.sem_inc(passed, 1)


def adaln_block_kernel(nc, x_tok, x_feat, setup_w, late_w, e_w1, e_wg, e_w2, e_b1, e_bg, out):
    ctx = ExitStack()
    with ctx:
        def sb(name, *shape, dtype=F32):
            return ctx.enter_context(nc.sbuf_tensor(name, [P, *shape], dtype))

        def sb_parts(name, *shape):
            return [sb(f"{name}_{part}", *shape, dtype=F32R) for part in ("high", "low")]

        def sem(name):
            return ctx.enter_context(nc.semaphore(name))

        x_in = sb("x_in", NS, TT, D)
        xres = sb("xres", NS, T)
        sw = sb("sw", SETUP_W)
        lw = sb("lw", LATE_W)
        conv_bd = sb("conv_bd", IC, K, P)
        w1 = sb("w1", S, F)
        wg = sb("wg", S, F)
        w2 = sb("w2", S, FC, D)
        b1, bg = (x_in[:, 8 * i:8 * i + 8, :, :].rearrange("p b i d -> p (b i d)")
                  .rearrange("p (g f) -> p g f", g=NG) for i in range(2))

        def carver(base):
            at = [0]

            def carve(*shape):
                a, b = at[0], at[0] + int(np.prod(shape))
                at[0] = b
                names = " ".join("abc"[:len(shape)])
                return base[:, a:b].rearrange(f"p ({names}) -> p {names}", **dict(zip("abc", shape)))
            return carve

        def part(name):
            a, b = SETUP_PARTS[name]
            return sw[:, a:b]

        def late(name):
            a, b = LATE_PARTS[name]
            return lw[:, a:b]

        def vec(name):
            a = SETUP_PARTS["vec"][0] + VEC[name]
            return sw[:, a:a + 1]

        ident = part("ident")
        conv_w = part("conv_w").rearrange("p (c k o) -> p c k o", c=IC, k=K)
        w_h = part("w_h").rearrange("p (c d) -> p c d", c=IC)
        w_gate = part("w_gate_t").rearrange("p (c d) -> p c d", c=IC)
        fc_t = part("fc_t").rearrange("p (c d) -> p c d", c=IC)
        out_t = part("out_t").rearrange("p (c d) -> p c d", c=IC)
        cproj = part("cproj").rearrange("p (c d) -> p c d", c=IC)
        wmod = part("wmod").rearrange("p (m d) -> p m d", m=6)
        mask_j = part("mask_j")
        mask_r = part("mask_r")

        c_tanh = sb("c_tanh", NS)
        c_silu = sb("c_silu", NS)
        mod = sb("mod", 6, NS)
        gate_sign = sb("gate_sign", 2, NS)
        gate_bias = sb("gate_bias", 2, NS)
        conv_m = sb_parts("conv_m", IC, K, P)
        w_gate_p = sb_parts("w_gate_p", IC, D)
        conv_bh = sb("conv_bh", IC)
        fc_g = sb("fc_g", IC, D)
        fc_c = sb("fc_c", IC, D)
        z_bias = sb("z_bias", 2)
        out_m = sb("out_m", D)
        slot_q = sb("slot_q", S)
        slot_bd = sb("slot_bd", H, S)
        key_q = sb("key_q", HC, P)
        key_b = sb("key_b", HC)
        slot_o = sb("slot_o", S)
        bias_o = sb("bias_o", 3)
        bq8 = sb("bq8", 1)
        means = sb("means", P)
        eps = sb("eps", TT)
        half_neg = sb("half_neg", TT)

        st1, mv1, ve1, rs1 = sb("st1", TT, 6), sb("mv1", TT, 2), sb("ve1", TT), sb("rs1", TT)
        sth, mvh, veh, rsh = sb("sth", TT, 6), sb("mvh", TT, 2), sb("veh", TT), sb("rsh", TT)
        st2, mv2, ve2, rs2 = sb("st2", TT, 6), sb("mv2", TT, 2), sb("ve2", TT), sb("rs2", TT)
        work = sb("work", 4096)
        carve = carver(work)
        n1 = carve(TT, D)
        hn_p = sb_parts("hn_p", K - 1 + T)
        hn_t = carve(T)
        g_tanh = carve(IC, T)
        g_silu2 = carve(IC, T)
        h = carve(IC, T)
        y_s = carve(TT, D)
        z = carve(T)
        z_tanh = carve(T)
        z_silu2 = carve(T)
        x1 = carve(T)
        n2 = carve(TT, D)
        h2_t = carve(T)
        q_t = sb("q_t", NS, T)
        val = sb("val", TT, D)
        mx = sb("mx", HC)
        mxb = sb("mxb", HC)
        ebias = sb("ebias", HC)
        prob = sb("prob", HC, T)
        prob_t = sb("prob_t", TT, HS)
        psum = sb("psum", HC)
        table_load = sb("table_load", 1)
        rsum = sb("rsum", HC)
        att_m = sb("att_m", HPC, S)
        att_t = sb("att_t", NS, S)
        o_t = sb("o_t", NS, S)
        st3, mv3, ve3, rs3 = sb("st3", 2, 6), sb("mv3", 2, 2), sb("ve3", 2), sb("rs3", 2)
        he_t = sb("he_t", S, Q)
        carve = carver(work)
        ub, gb_, us, gs = (carve(2, F) for _ in range(4))
        n3 = gs[:, 0, 0:2 * D].rearrange("p (i d) -> p i d", i=2)
        ng3 = gs[:, 1, 0:NS * S].rearrange("p (b s) -> p b s", b=NS)
        ug = conv_bd[:, :, :, :].rearrange("p c k o -> p c (k o)")
        at = SETUP_PARTS["w_h"][0]
        ug_t = sw[:, at:at + 2 * FC * P].rearrange("p (g k o) -> p g k o", g=2, k=FC)
        ye = sw[:, at + 2 * FC * P:at + 2 * FC * P + 2 * D].rearrange("p (g d) -> p g d", g=2)
        o2_t = part("w_gate_t").rearrange("p (b s) -> p b s", b=NS)
        k2_t = sb("k2_t", NS, S)
        carve = carver(work)
        q_s = carve(T)
        k2_bd = carve(H, S)
        v2t_bd = carve(H, S)
        v2_t = carve(NS, S)
        v2w = carve(HC, D)
        e2_of = [carve(TT, HS) for _ in range(2)]
        p2 = carve(TT, HS)
        y2g = carve(T)
        mx2 = sb("mx2", TT, H)
        sum2 = sb("sum2", TT, H)
        rsum2 = sb("rsum2", TT, H)
        s2_rows, p2_t = prob, prob_t

        ps = ctx.enter_context(nc.psum_tensor("ps", [P, 8, 512], F32))

        def bank(n, *shape):
            width = int(np.prod(shape))
            v = ps[:, n, 0:width]
            if len(shape) == 2:
                v = v.rearrange("p (a b) -> p a b", a=shape[0])
            return v

        gate_ps = bank(0, IC, T)
        conv_ps = (bank(1, T), ps[:, 5, T:2 * T])
        hT_ps = bank(2, TT, I)
        pT_ps = bank(3, TT, HS)
        s_ps = bank(3, HC, T)
        av_ps = ps[:, 4, T:T + P].rearrange("p (h s) -> p h s", s=S)
        y_ps = bank(4, TT, D)
        out_ps = bank(4, T)
        yT_ps = bank(5, T)
        hn_ps = bank(5, T)
        x1_ps = bank(6, TT, D)
        n2_ps = bank(6, T)
        q_ps = ps[:, 7, 0:T]
        v_ps = ps[:, 7, T:2 * T].rearrange("p (a b) -> p a b", a=TT)

        def by_head(x):
            return x.rearrange("p (h s) -> p h s", s=S)

        s2_ps_of = [bank(0, TT, HS), bank(6, TT, HS)]

        setup_in = [sem(f"setup_in{i}") for i in range(3)]
        x_in_sem = [sem(f"x_in{i}") for i in range(4)]
        xres_in = sem("xres_in")
        late_in = sem("late_in")
        expert_in = sem("expert_in")
        zeroed = sem("zeroed")
        means_ok = sem("means_ok")
        conv_bd_ok = sem("conv_bd_ok")
        conv_m_ok = sem("conv_m_ok")
        mod_ok = sem("mod_ok")
        gate_high_ok, conv_low_ok = sem("gate_high_ok"), sem("conv_low_ok")
        fc_c_ok = sem("fc_c_ok")
        (c_tanh_ok, c_ready, conv_m_mm, slot_q_mm, mod_mm, fc_g_ok, fc_mean_mm, slot_bd_ok, key_q_mm, out_m_mm,
         bias_mm, dve_chain) = (sem(n) for n in [
             "c_tanh_ok", "c_ready", "conv_m_mm", "slot_q_mm", "mod_mm", "fc_g_ok", "fc_mean_mm", "slot_bd_ok",
             "key_q_mm", "out_m_mm", "bias_mm", "dve_chain"])
        setup_done_dve = sem("setup_done_dve")
        setup_done_act = sem("setup_done_act")
        pool_ready = sem("pool_ready")
        ev = {n: sem(n) for n in [
            "st1_ok", "mv1_ok", "ve1_ok", "rs1_ok", "n1_ok", "hn_mm", "hn_ok", "hnhigh_ok", "hnlow_ok", "gate_mm",
            "gtanh_ok", "gsilu_ok", "conv0_mm", "conv_mm", "h_ok", "hT_mm", "y_mm", "sth_ok", "mvh_ok", "veh_ok", "rsh_ok",
            "ys_ok", "yT_mm", "ztanh_ok", "zsilu_ok", "h0_used", "out_mm", "xb_ok", "x1_ok", "x1_kept", "x1_mm", "st2_ok", "mv2_ok", "ve2_ok",
            "rs2_ok", "n2_ok", "n2_mm", "h2_ok", "s_mm", "mx_ok", "mxb_ok", "ebias_ok", "exp_ok", "rsum_ok", "prob_ok", "qv_mm",
            "qv_ok", "pT_mm", "pT_ok",
            "av_mm", "attm_ok", "at_ok"]}
        o_mm, o_ok, oT_mm, e_chain, e_pool, eT_mm, he_ok = (sem(n) for n in [
            "o_mm", "o_ok", "oT_mm", "e_chain", "e_pool", "eT_mm", "he_ok"])
        u_mm, ub_ok, us_ok, ug_ok, ugT_mm, ugT_ok, ye_mm, ye_ok, yeT_mm, o2_ok, k2_mm, k2_ok = (sem(n) for n in [
            "u_mm", "ub_ok", "us_ok", "ug_ok", "ugT_mm", "ugT_ok", "ye_mm", "ye_ok", "yeT_mm", "o2_ok", "k2_mm",
            "k2_ok"])
        f = {n: sem("f_" + n) for n in [
            "k2bd_ok", "qs_ok", "v2bd_ok", "v2w_mm", "v2w_ok", "s2_mm", "mx2_ok", "s2_half", "s2_ok", "e2_half",
            "e2_ok", "sum2_ok", "rsum2_ok",
            "p2_half", "p2_ok", "p2T_mm", "p2T_ok", "y2_mm", "y2g_ok", "xo_ok"]}
        v2_mm, v2_ok = sem("v2_mm"), sem("v2_ok")
        stored = sem("stored")
        act_passed, dve_passed, pool_passed = sem("act_passed"), sem("dve_passed"), sem("pool_passed")

        block = ctx.enter_context(nc.Block())

        FIRST, LAST = -2, NS + 1
        LOOP = (2, NS - 2)
        LOOP2 = (4, NS - 2, 2)
        LAST2 = NS + 2

        @block.sync
        def _(sp):
            def load_setup(i):
                c = slice(SETUP_LOADS[i], SETUP_LOADS[i + 1])
                sp.dma_start(sw[:, c], setup_w[:, c]).then_inc(setup_in[i], 16)

            def load_x(i):
                b = slice(X_LOADS[i], X_LOADS[i + 1])
                sp.dma_start(x_in[:, b, :, :], x_tok[:, b, :, :]).then_inc(x_in_sem[i], 16)

            load_setup(0)
            load_x(0)
            load_setup(1)
            load_setup(2)
            for i in range(1, 4):
                load_x(i)
            sp.dma_start(xres[:, :, :], x_feat).then_inc(xres_in, 16)
            sp.dma_start(lw[:, :], late_w).then_inc(late_in, 16)
            for e in range(0, S, 4):
                sp.dma_start(w1[:, e:e + 4, :], e_w1[:, e:e + 4, :]).then_inc(expert_in, 16)
                sp.dma_start(wg[:, e:e + 4, :], e_wg[:, e:e + 4, :]).then_inc(expert_in, 16)
                sp.dma_start(w2[:, e:e + 4, :, :], e_w2[:, e:e + 4, :, :]).then_inc(expert_in, 16)
            sp.wait_ge(ev["n1_ok"], NS)
            for src, dst in ((e_b1, b1), (e_bg, bg)):
                for j in range(EG):
                    sp.dma_start(dst[Q * j:Q * j + Q, :, :],
                                 src.rearrange("(g j) f -> j g f", j=EG)[j:j + 1].broadcast_to([Q, NG, F])
                                 ).then_inc(expert_in, 16)
            with sp.Fori(0, NS) as t:
                sp.wait_ge(f["xo_ok"], t + 1)
                sp.dma_start(out[:, bass.ds(t, 1), :], xres[:, bass.ds(t, 1), :]).then_inc(stored, 16)
            sp.wait_ge(stored, 16 * NS)
        EXPERT_LOADS = 16 * (2 * EG + 3 * (S // 4))

        @block.gpsimd
        def _(pool):
            nc.gpsimd.memset(means[:, :], 1.0 / I).then_inc(means_ok, 1)
            nc.gpsimd.memset(conv_bd[:, :, :, :], 0.0).then_inc(zeroed, 1)
            nc.gpsimd.memset(eps[:, :], EPS)
            nc.gpsimd.memset(half_neg[:, :], -0.5)
            for x in hn_p:
                nc.gpsimd.memset(x[:, 0:K - 1].bitcast(F32), 0.0)
            nc.gpsimd.memset(he_t[:, :, :], 0.0).then_inc(pool_ready, 1)

            def rsqrt(mv, ve, rs, mv_ok, ve_ok, rs_ok, b):
                wait(pool, mv_ok, b + 1)
                nc.gpsimd.tensor_tensor(ve[:, :], mv[:, :, 1], eps[:, :], ALU.add).then_inc(ve_ok, 1)
                wait(pool, ve_ok, b + 1)
                nc.gpsimd.tensor_tensor(rs[:, :], ve[:, :], half_neg[:, :], ALU.pow).then_inc(rs_ok, 1)

            def slot(t):
                if exists(t):
                    xs = xres[:, bass.ds(t, 1), :].rearrange("p a t -> p (a t)")
                    nc.gpsimd.tensor_tensor(xs, xs, gate_bias[:, 0, bass.ds(t, 1)].broadcast_to([P, T]),
                                            ALU.add).then_inc(ev["xb_ok"], 1)
                if exists(t):
                    rsqrt(mvh, veh, rsh, ev["mvh_ok"], ev["veh_ok"], ev["rsh_ok"], t)
                if exists(t + 2):
                    rsqrt(mv1, ve1, rs1, ev["mv1_ok"], ev["ve1_ok"], ev["rs1_ok"], t + 2)
                if exists(t):
                    wait_alone(pool, ev["x1_ok"], t + 1, pool_passed)
                    xs = xres[:, bass.ds(t, 1), :].rearrange("p a t -> p (a t)")
                    nc.gpsimd.tensor_copy(xs, x1[:, :]).then_inc(ev["x1_kept"], 1)
                if exists(t):
                    rsqrt(mv2, ve2, rs2, ev["mv2_ok"], ev["ve2_ok"], ev["rs2_ok"], t)

            pool.wait_ge(pool_ready, 1)
            for t in range(FIRST, 0):
                slot(t)
            pool.wait_ge(xres_in, 16)
            pool.wait_ge(setup_done_dve, 1)
            for t in range(0, LOOP[0]):
                slot(t)
            with pool.Fori(*LOOP) as t:
                slot(t)
            for t in range(LOOP[1], LAST + 1):
                slot(t)

            pool.wait_ge(e_chain, 2)
            nc.gpsimd.tensor_tensor(ve3[:, :], mv3[:, :, 1], eps[:, :], ALU.add).then_inc(e_pool, 1)
            pool.wait_ge(e_pool, 1)
            nc.gpsimd.tensor_tensor(rs3[:, :], ve3[:, :], half_neg[:, :], ALU.pow).then_inc(e_pool, 1)

            def keys(t):
                wait_alone(pool, f["s2_mm"], t, pool_passed)
                kb = k2_t[:, bass.ds(t, 1), :].broadcast_to([P, H, S])
                nc.gpsimd.tensor_tensor(k2_bd[:, :, :], kb, mask_j.unsqueeze(2).broadcast_to([P, H, S]),
                                        ALU.mult).then_inc(f["k2bd_ok"], 1)

            def values(t):
                if first(t):
                    pool.wait_ge(v2_ok, 1)
                wait_alone(pool, f["v2w_mm"], t, pool_passed)
                vb = v2_t[:, bass.ds(t, 1), :].broadcast_to([P, H, S])
                nc.gpsimd.tensor_tensor(v2t_bd[:, :, :], vb, mask_j.unsqueeze(2).broadcast_to([P, H, S]),
                                        ALU.mult).then_inc(f["v2bd_ok"], 1)

            def probs2(t, parity):
                wait(pool, f["rsum2_ok"], t + 1)
                wait(pool, f["p2T_mm"], t)
                nc.gpsimd.tensor_tensor(by_head(p2[:, 1, :]), by_head(e2_of[parity][:, 1, :]),
                                        rsum2[:, 1, :].unsqueeze(2).broadcast_to([P, H, S]),
                                        ALU.mult).then_inc(f["p2_ok"], 1)

            def residual2(t):
                wait_alone(pool, f["y2g_ok"], t + 1, pool_passed)
                xs = xres[:, bass.ds(t, 1), :].rearrange("p a t -> p (a t)")
                nc.gpsimd.tensor_tensor(xs, xs, y2g[:, :], ALU.add).then_inc(f["xo_ok"], 1)

            def slot2(t, parity):
                if exists(t + 1):
                    keys(t + 1)
                if exists(t - 3):
                    residual2(t - 3)
                if exists(t - 1):
                    probs2(t - 1, 1 - parity)
                    values(t - 1)

            pool.wait_ge(k2_ok, 1)
            keys(0)
            for t in range(0, LOOP2[0]):
                slot2(t, t % 2)
            with pool.Fori(*LOOP2) as t:
                slot2(t, LOOP2[0] % 2)
                slot2(t + 1, (LOOP2[0] + 1) % 2)
            for t in range(LOOP2[1], LAST2 + 1):
                slot2(t, t % 2)

        @block.scalar
        def _(act):
            act.wait_ge(setup_in[0], 16)
            nc.scalar.activation(c_tanh[:, :], part("c_t"), ACT.Tanh, scale=0.5).then_inc(c_tanh_ok, 1)
            for c in range(IC):
                act.wait_ge(conv_m_mm, 1 + c)
                nc.scalar.mul(conv_m[0][:, c, :, :], bank(1 + c, K, P), 0.5).then_inc(conv_m_ok, 1)

            def modulated(dst, src, scale_at, shift_at, b):
                return nc.scalar.activation(dst, src, ACT.Identity, bias=mod[:, shift_at, bass.ds(b, 1)],
                                            scale=mod[:, scale_at, bass.ds(b, 1)])

            def slot(t):
                if exists(t + 1):
                    wait_alone(act, ev["hn_mm"], t + 2, act_passed)
                    modulated(hn_t[:, :], hn_ps, 1, 0, t + 1).then_inc(ev["hn_ok"], 1)
                if exists(t - 2):
                    wait(act, ev["pT_mm"], t - 1)
                    nc.scalar.copy(prob_t[:, :, :], pT_ps).then_inc(ev["pT_ok"], 1)
                if exists(t + 1):
                    wait(act, ev["gate_mm"], t + 2)
                    nc.scalar.activation(g_tanh[:, :, :], gate_ps, ACT.Tanh, scale=0.5).then_inc(ev["gtanh_ok"], 1)
                if exists(t):
                    wait(act, ev["rsh_ok"], t + 1)
                    wait(act, ev["y_mm"], t + 1)
                    wait(act, ev["attm_ok"], t - 1)
                    wait(act, ev["yT_mm"], t)
                    for i in range(TT):
                        ins = nc.scalar.activation(y_s[:, i, :], y_ps[:, i, :], ACT.Identity, scale=rsh[:, i:i + 1])
                    ins.then_inc(ev["ys_ok"], 1)
                if exists(t - 1):
                    wait_alone(act, ev["n2_mm"], t, act_passed)
                    modulated(h2_t[:, :], n2_ps, 4, 3, t - 1).then_inc(ev["h2_ok"], 1)
                if exists(t):
                    if first(t):
                        act.wait_ge(setup_done_dve, 1)
                    wait(act, ev["yT_mm"], t + 1)
                    nc.scalar.activation(z[:, :], yT_ps, ACT.Identity, bias=z_bias[:, 0:1])
                    nc.scalar.activation(z_tanh[:, :], yT_ps, ACT.Tanh, bias=z_bias[:, 1:2],
                                         scale=0.5).then_inc(ev["ztanh_ok"], 1)
                if exists(t - 1):
                    wait(act, ev["ebias_ok"], t)
                    for c in range(HC):
                        ins = nc.scalar.activation(prob[:, c, :], s_ps[:, c, :], ACT.Exp, bias=ebias[:, c:c + 1],
                                                   accum_out=psum[:, c:c + 1])
                    ins.then_inc(ev["exp_ok"], 1)
                if exists(t - 1):
                    wait_alone(act, ev["qv_mm"], t, act_passed)
                    nc.scalar.copy(val[:, :, :], v_ps)
                    nc.scalar.activation(q_t[:, bass.ds(t - 1, 1), :].rearrange("p a t -> p (a t)"), q_ps, ACT.Identity,
                                         bias=bq8[:, :], scale=R8).then_inc(ev["qv_ok"], 1)

            act.wait_ge(mod_ok, 1)
            for t in range(FIRST, 0):
                slot(t)
            act.wait_ge(key_q_mm, 1)
            nc.scalar.copy(key_q[:, :, :], bank(6, HC, P))
            act.wait_ge(out_m_mm, 1)
            nc.scalar.mul(out_m[:, :], bank(7, D), 0.5).then_inc(setup_done_act, 1)
            for t in range(0, LOOP[0]):
                slot(t)
            with act.Fori(*LOOP) as t:
                slot(t)
            for t in range(LOOP[1], LAST + 1):
                slot(t)

            nc.scalar.activation(table_load[:, :], eps[:, 0:1], ACT.Silu)

            def silus(g):
                act.wait_ge(ub_ok, 2 * g + 1)
                nc.scalar.activation(us[:, g % 2, :], ub[:, g % 2, :], ACT.Silu)
                act.wait_ge(ub_ok, 2 * g + 2)
                if g >= 2:
                    act.wait_ge(ug_ok, g - 1)
                nc.scalar.activation(gs[:, g % 2, :], gb_[:, g % 2, :], ACT.Silu).then_inc(us_ok, 1)

            def hidden_t(g):
                act.wait_ge(ugT_mm, g + 1)
                if g >= 2:
                    act.wait_ge(ye_mm, g - 1)
                nc.scalar.copy(ug_t[:, g % 2, :, :], bank(2, FC, P)).then_inc(ugT_ok, 1)

            def outputs(g):
                act.wait_ge(ye_mm, g + 1)
                nc.scalar.copy(ye[:, g % 2, :], bank(3, D)).then_inc(ye_ok, 1)

            for g in range(NG + 2):
                if g < NG:
                    silus(g)
                if g >= 2:
                    outputs(g - 2)
                if 1 <= g < NG + 1:
                    hidden_t(g - 1)

            nc.scalar.activation(table_load[:, :], eps[:, 0:1], ACT.Exp)
            halves2 = (("s2_half", "p2_half", "e2_half"), ("s2_ok", "p2_ok", "e2_ok"))

            def queries2(b):
                wait_alone(act, f["s2_mm"], b, act_passed)
                nc.scalar.copy(q_s[:, :], q_t[:, bass.ds(b, 1), :].rearrange("p a t -> p (a t)")
                               ).then_inc(f["qs_ok"], 1)

            def slot2(t, parity):
                if exists(t + 1):
                    queries2(t + 1)
                if exists(t - 3):
                    wait_alone(act, f["y2_mm"], t - 2, act_passed)
                    wait_alone(act, f["xo_ok"], t - 3, act_passed)
                    nc.scalar.activation(y2g[:, :], bank(4, T), ACT.Identity, bias=gate_bias[:, 1, bass.ds(t - 3, 1)],
                                         scale=mod[:, 5, bass.ds(t - 3, 1)]).then_inc(f["y2g_ok"], 1)
                if exists(t - 2):
                    wait(act, f["p2T_mm"], t - 1)
                    wait(act, f["y2_mm"], t - 2)
                    nc.scalar.copy(p2_t[:, :, :], bank(1, HC, T)).then_inc(f["p2T_ok"], 1)
                    wait(act, f["v2w_mm"], t - 1)
                    nc.scalar.copy(v2w[:, :, :], bank(5, HC, D)).then_inc(f["v2w_ok"], 1)
                if exists(t):
                    for i in range(TT):
                        shifted, used, made = halves2[i]
                        wait(act, f[shifted], t + 1)
                        wait(act, f[used], t - 1)
                        nc.scalar.activation(e2_of[parity][:, i, :], s2_rows[:, i, :], ACT.Exp).then_inc(f[made], 1)

            queries2(0)
            for t in range(0, LOOP2[0]):
                slot2(t, t % 2)
            with act.Fori(*LOOP2) as t:
                slot2(t, LOOP2[0] % 2)
                slot2(t + 1, (LOOP2[0] + 1) % 2)
            for t in range(LOOP2[1], LAST2 + 1):
                slot2(t, t % 2)

        @block.tensor
        def _(pe):
            def mm(dst, lhs, rhs, first=True, last=True):
                return nc.tensor.matmul(dst, lhs, rhs, start=first, stop=last)

            def flip(dst, src):
                return nc.tensor.transpose(dst, src, ident)

            PARTS = ((0, 0), (1, 0), (0, 1))

            def keep_warm(n, b=7, x=ident):
                for _ in range(n):
                    mm(bank(b, P), x, x)

            pe.wait_ge(means_ok, 1)
            keep_warm(9, 7, means[:, :])
            pe.wait_ge(conv_bd_ok, IC)
            for c in range(IC):
                mm(ps[:, 1 + c, :], w_h[:, c, :], conv_bd[:, c, :, :]).then_inc(conv_m_mm, 1)
            pe.wait_ge(c_ready, 1)
            pe.wait_ge(setup_in[1], 16)
            for m in range(6):
                ins = mm(ps[:, 0, m * NS:(m + 1) * NS], wmod[:, m, :], c_silu[:, :])
            ins.then_inc(mod_mm, 1)
            mm(bank(7, S), part("d_wq"), part("slot_t")).then_inc(slot_q_mm, 1)

            def keep_warm_at_the_end(b, n):
                if isinstance(b, int) and b == NS - 1:
                    keep_warm(n, 0)

            def norm_to_features(b):
                wait(pe, ev["n1_ok"], b + 1)
                wait(pe, ev["h_ok"], b)
                for i in range(TT):
                    ins = flip(hn_ps[:, i * P:(i + 1) * P], n1[:, i, :])
                ins.then_inc(ev["hn_mm"], 1)

            def gate(b):
                if first(b):
                    keep_warm(4, 6)
                wait(pe, ev["hnlow_ok"], b + 1)
                wait(pe, ev["gsilu_ok"], b)
                for c in range(IC):
                    for n, (wp, xp) in enumerate(PARTS):
                        ins = mm(gate_ps[:, c, :], w_gate_p[wp][:, c, :], hn_p[xp][:, K - 1:K - 1 + T], n == 0,
                                 n == len(PARTS) - 1)
                ins.then_inc(ev["gate_mm"], 1)

            def conv(b, c, taps):
                if c == 0 and taps[0] == 0:
                    wait(pe, ev["h_ok"], b)
                for k in taps:
                    for n, (wp, xp) in enumerate(PARTS):
                        ins = mm(conv_ps[c], conv_m[wp][:, c, k, :], hn_p[xp][:, k:k + T], k == 0 and n == 0,
                                 k == K - 1 and n == len(PARTS) - 1)
                if taps[-1] == K - 1:
                    ins.then_inc(ev["conv_mm"] if c == IC - 1 else ev["conv0_mm"], 1)

            def inner_to_tokens(b):
                wait(pe, ev["h_ok"], b + 1)
                wait(pe, ev["sth_ok"], b)
                for i in range(TT):
                    for c in range(IC):
                        ins = flip(hT_ps[:, i, c * P:(c + 1) * P], h[:, c, i * P:(i + 1) * P])
                ins.then_inc(ev["hT_mm"], 1)

            def inner_product(b):
                wait(pe, ev["x1_ok"], b)
                for i in range(TT):
                    for c in range(IC):
                        ins = mm(y_ps[:, i, :], h[:, c, i * P:(i + 1) * P], fc_c[:, c, :], c == 0, c == IC - 1)
                ins.then_inc(ev["y_mm"], 1)

            def inner_to_features(b):
                wait(pe, ev["ys_ok"], b + 1)
                wait(pe, ev["hn_ok"], b + 2)
                for i in range(TT):
                    ins = flip(yT_ps[:, i * P:(i + 1) * P], y_s[:, i, :])
                ins.then_inc(ev["yT_mm"], 1)

            def project_out(b):
                if first(b):
                    keep_warm(6, 6)
                    pe.wait_ge(setup_done_act, 1)
                wait(pe, ev["zsilu_ok"], b + 1)
                for c in range(IC):
                    ins = mm(out_ps, out_t[:, c, :], h[:, c, :], c == 0, False)
                    if c == 0:
                        ins.then_inc(ev["h0_used"], 1)
                mm(out_ps, out_m[:, :], z_silu2[:, :], False, True).then_inc(ev["out_mm"], 1)

            def residual_to_tokens(b):
                keep_warm_at_the_end(b, 2)
                wait(pe, ev["x1_ok"], b + 1)
                wait(pe, ev["h2_ok"], b)
                for i in range(TT):
                    ins = flip(x1_ps[:, i, :], x1[:, i * P:(i + 1) * P])
                ins.then_inc(ev["x1_mm"], 1)

            def norm2_to_features(b):
                keep_warm_at_the_end(b, 3)
                wait(pe, ev["n2_ok"], b + 1)
                for i in range(TT):
                    ins = flip(n2_ps[:, i * P:(i + 1) * P], n2[:, i, :])
                ins.then_inc(ev["n2_mm"], 1)

            def scores(b):
                keep_warm_at_the_end(b, 4)
                wait(pe, ev["h2_ok"], b + 1)
                wait(pe, ev["pT_ok"], b)
                for c in range(HC):
                    ins = mm(s_ps[:, c, :], key_q[:, c, :], h2_t[:, :])
                ins.then_inc(ev["s_mm"], 1)

            def queries_values(b):
                wait(pe, ev["qv_ok"], b)
                mm(q_ps, part("c_wq"), h2_t[:, :])
                for i in range(TT):
                    ins = mm(v_ps[:, i, :], h2_t[:, i * P:(i + 1) * P], part("d_wv"))
                ins.then_inc(ev["qv_mm"], 1)

            def prob_to_tokens(b):
                keep_warm_at_the_end(b, 6)
                wait(pe, ev["prob_ok"], b + 1)
                for i in range(TT):
                    for c in range(HC):
                        ins = flip(pT_ps[:, i, c * P:(c + 1) * P], prob[:, c, i * P:(i + 1) * P])
                ins.then_inc(ev["pT_mm"], 1)

            def attend(b):
                keep_warm_at_the_end(b, 4)
                wait(pe, ev["pT_ok"], b + 1)
                wait(pe, ev["qv_ok"], b + 1)
                wait(pe, ev["x1_ok"], b + 2)
                for i in range(TT):
                    for c in range(HC):
                        j = slice(c * JC, (c + 1) * JC)
                        ins = mm(av_ps[j], val[:, i, j], prob_t[:, i, c * P:(c + 1) * P], i == 0, i == TT - 1)
                ins.then_inc(ev["av_mm"], 1)

            def slot(t):
                if exists(t + 1):
                    norm_to_features(t + 1)
                if exists(t):
                    inner_to_tokens(t)
                if exists(t):
                    inner_product(t)
                if exists(t - 2):
                    attend(t - 2)
                if exists(t + 1):
                    gate(t + 1)
                if exists(t + 1):
                    conv(t + 1, 0, range(0, K // 2))
                if exists(t - 1):
                    norm2_to_features(t - 1)
                if exists(t + 1):
                    conv(t + 1, 0, range(K // 2, K))
                if exists(t):
                    inner_to_features(t)
                if exists(t - 1):
                    scores(t - 1)
                if exists(t - 1):
                    queries_values(t - 1)
                if exists(t):
                    project_out(t)
                if exists(t + 1):
                    conv(t + 1, 1, range(0, K // 2))
                if exists(t + 1):
                    conv(t + 1, 1, range(K // 2, K))
                if exists(t):
                    residual_to_tokens(t)
                if exists(t - 1):
                    prob_to_tokens(t - 1)

            pe.wait_ge(conv_low_ok, IC)
            for t in range(FIRST, 0):
                slot(t)
            pe.wait_ge(setup_in[2], 16)
            pe.wait_ge(fc_g_ok, 1)
            for c in range(IC):
                ins = mm(bank(3, D), means[:, :], fc_g[:, c, :], c == 0, c == IC - 1)
            ins.then_inc(fc_mean_mm, 1)
            pe.wait_ge(slot_bd_ok, 1)
            mm(bank(6, HS), part("d_wk_t"), slot_bd[:, :, :]).then_inc(key_q_mm, 1)
            for c in range(IC):
                ins = mm(bank(7, D), cproj[:, c, :], out_t[:, c, :], c == 0, c == IC - 1)
            ins.then_inc(out_m_mm, 1)
            pe.wait_ge(fc_c_ok, 1)
            for c in range(IC):
                mm(ps[:, 3, 0:1], fc_t[:, c, :], vec(f"ln_b{c}"), c == 0, c == IC - 1)
            for c in range(IC):
                mm(ps[:, 3, 1:2], out_t[:, c, :], vec(f"cproj_b{c}"), c == 0, c == IC - 1)
            for c in range(HC):
                mm(ps[:, 3, 2 + c:3 + c], slot_bd[:, c * HPC:(c + 1) * HPC, :], vec("d_bk"))
            mm(ps[:, 3, 4:5], part("d_wo"), vec("d_bv"))
            mm(ps[:, 3, 5:6], part("c_wo"), vec("c_bv")).then_inc(bias_mm, 1)
            for t in range(0, LOOP[0]):
                slot(t)
            with pe.Fori(*LOOP) as t:
                slot(t)
            for t in range(LOOP[1], LAST + 1):
                slot(t)

            keep_warm(3)
            pe.wait_ge(ev["at_ok"], NS)
            pe.wait_ge(late_in, 16)
            pe.wait_ge(expert_in, EXPERT_LOADS)
            mm(bank(0, NS * S), part("d_wo"), att_t[:, :, :]).then_inc(o_mm, 1)
            keep_warm(3)
            pe.wait_ge(o_ok, 1)
            for i in range(2):
                ins = flip(ps[:, 1, i * P:(i + 1) * P], o_t[:, i * NS // 2:(i + 1) * NS // 2, :])
            ins.then_inc(oT_mm, 1)
            keep_warm(12)
            pe.wait_ge(e_chain, 3)
            for i in range(2):
                ins = flip(ps[:, 2, i * P:(i + 1) * P], n3[:, i, :])
            ins.then_inc(eT_mm, 1)
            keep_warm(5)
            pe.wait_ge(he_ok, 1)

            def hidden(g):
                for n, w in ((4, w1), (6, wg)):
                    if g >= 2:
                        pe.wait_ge(ub_ok, 2 * (g - 2) + (1 if n == 4 else 2))
                    for j in range(EG):
                        ins = mm(ps[Q * j:Q * j + Q, n + g % 2, :], he_t[:, EG * g + j, :], w[:, EG * g + j, :])
                    ins.then_inc(u_mm, 1)

            def hidden_to_rows(g):
                if g >= 1:
                    pe.wait_ge(ugT_ok, g)
                keep_warm(6 if g == 0 else 1, 2)
                pe.wait_ge(ug_ok, g + 1)
                for k in range(FC):
                    ins = flip(ps[:, 2, k * P:(k + 1) * P], ug[:, g % 2, k * P:(k + 1) * P])
                ins.then_inc(ugT_mm, 1)

            def hidden_product(g):
                if g >= 1:
                    pe.wait_ge(ye_ok, g)
                if g >= 2:
                    keep_warm(2, 3)
                pe.wait_ge(ugT_ok, g + 1)
                for k in range(FC):
                    for j in range(EG):
                        ins = mm(ps[Q * j:Q * j + Q, 3, 0:D], ug_t[:, g % 2, k, Q * j:Q * j + Q],
                                 w2[:, EG * g + j, k, :], k == 0, k == FC - 1)
                ins.then_inc(ye_mm, 1)

            def to_slots(g):
                pe.wait_ge(ye_ok, g + 1)
                if g >= 2:
                    pe.wait_ge(o2_ok, g - 1)
                flip(ps[:, g % 2, 0:P], ye[:, g % 2, :]).then_inc(yeT_mm, 1)

            for g in range(NG + 3):
                if g < NG:
                    hidden(g)
                if 2 <= g < NG + 2:
                    hidden_product(g - 2)
                if 1 <= g < NG + 1:
                    hidden_to_rows(g - 1)
                if 3 <= g < NG + 3:
                    to_slots(g - 3)
            keep_warm(2)
            pe.wait_ge(o2_ok, NG)
            mm(bank(4, NS * S), late("c_wk"), o2_t[:, :, :]).then_inc(k2_mm, 1)
            mm(bank(5, NS * S), late("c_wv"), o2_t[:, :, :]).then_inc(v2_mm, 1)

            def scores2(b, parity):
                wait(pe, f["k2bd_ok"], b + 1)
                wait(pe, f["qs_ok"], b + 1)
                wait(pe, f["s2_ok"], b - 1)
                for i in range(TT):
                    ins = mm(s2_ps_of[parity][:, i, :], q_s[:, i * P:(i + 1) * P], k2_bd[:, :, :])
                ins.then_inc(f["s2_mm"], 1)

            def probs2_to_rows(b):
                wait(pe, f["p2_half"], b + 1)
                wait(pe, f["p2_ok"], b + 1)
                wait(pe, f["p2T_ok"], b)
                for c in range(HC):
                    for i in range(TT):
                        ins = flip(ps[:, 1, c * T + i * P:c * T + (i + 1) * P], p2[:, i, c * P:(c + 1) * P])
                ins.then_inc(f["p2T_mm"], 1)

            def values2(b):
                wait(pe, f["v2bd_ok"], b + 1)
                wait(pe, f["v2w_ok"], b)
                for c in range(HC):
                    ins = mm(ps[:, 5, c * D:(c + 1) * D], v2t_bd[:, c * HPC:(c + 1) * HPC, :], part("c_wo"))
                ins.then_inc(f["v2w_mm"], 1)

            def outputs2(b):
                wait(pe, f["p2T_ok"], b + 1)
                wait(pe, f["v2w_ok"], b + 1)
                wait(pe, f["y2g_ok"], b)
                for c in range(HC):
                    ins = mm(bank(4, T), v2w[:, c, :], p2_t[:, c, :], c == 0, c == HC - 1)
                ins.then_inc(f["y2_mm"], 1)

            def slot2(t, parity):
                if exists(t):
                    scores2(t, parity)
                if exists(t - 3):
                    outputs2(t - 3)
                if exists(t - 2):
                    probs2_to_rows(t - 2)
                    values2(t - 2)

            for t in range(0, LOOP2[0]):
                if t <= 2:
                    keep_warm(4)
                slot2(t, t % 2)
            with pe.Fori(*LOOP2) as t:
                slot2(t, LOOP2[0] % 2)
                slot2(t + 1, (LOOP2[0] + 1) % 2)
            for t in range(LOOP2[1], LAST2 + 1):
                slot2(t, t % 2)

        @block.vector
        def _(dve):
            v = nc.vector
            links = [0]

            def chain(ins):
                links[0] += 1
                ins.then_inc(dve_chain, 1)
                dve.wait_ge(dve_chain, links[0])

            def over_samples(x):
                return x.unsqueeze(1).broadcast_to([P, NS, S])

            dve.wait_ge(setup_in[0], 16)
            dve.wait_ge(zeroed, 1)
            for c in range(IC):
                for q in range(P // CG):
                    r = slice(q * CG, (q + 1) * CG)
                    ins = v.tensor_copy(conv_bd[r, c, :, r], conv_w[r, c, :, :])
                ins.then_inc(conv_bd_ok, 1)
            dve.wait_ge(c_tanh_ok, 1)
            chain(v.scalar_tensor_tensor(out=c_silu[:, :], in0=c_tanh[:, :], scalar=1.0, in1=part("c_t"),
                                         op0=ALU.add, op1=ALU.mult))
            v.tensor_scalar(c_silu[:, :], c_silu[:, :], 0.5, None, ALU.mult).then_inc(c_ready, 1)

            def setup_of_first_slots():
                dve.wait_ge(setup_in[1], 16)
                v.tensor_copy(w_gate_p[0][:, :, :], w_gate).then_inc(gate_high_ok, 1)
                dve.wait_ge(gate_high_ok, 1)
                v.tensor_tensor(w_gate_p[1][:, :, :], w_gate, w_gate_p[0][:, :, :].bitcast(F32), ALU.subtract)
                for c in range(IC):
                    dve.wait_ge(conv_m_ok, c + 1)
                    v.scalar_tensor_tensor(out=conv_m[1][:, c, :, :], in0=bank(1 + c, K, P), scalar=0.5,
                                           in1=conv_m[0][:, c, :, :].bitcast(F32), op0=ALU.mult,
                                           op1=ALU.subtract).then_inc(conv_low_ok, 1)
                dve.wait_ge(mod_mm, 1)
                chain(v.tensor_copy(mod[:, :, :], bank(0, 6, NS)))
                for m in (1, 4):
                    ins = v.tensor_scalar(mod[:, m, :], mod[:, m, :], 1.0, None, ALU.add)
                ins.then_inc(mod_ok, 1)
                dve.wait_ge(slot_q_mm, 1)
                chain(v.tensor_scalar(slot_q[:, :], bank(7, S), vec("d_bq"), R8, ALU.add, ALU.mult))
                v.tensor_tensor(slot_bd[:, :, :], mask_j.unsqueeze(2).broadcast_to([P, H, S]),
                                slot_q[:, :].unsqueeze(1).broadcast_to([P, H, S]), ALU.mult).then_inc(slot_bd_ok, 1)
                v.tensor_scalar(bq8[:, :], vec("c_bq"), R8, None, ALU.mult)
                for c in range(IC):
                    v.tensor_scalar(conv_bh[:, c:c + 1], vec(f"conv_b{c}"), 0.5, None, ALU.mult)

            def setup_of_later_steps():
                dve.wait_ge(setup_in[2], 16)
                for c in range(IC):
                    ins = v.tensor_scalar(fc_g[:, c, :], fc_t[:, c, :], vec(f"ln_g{c}"), None, ALU.mult)
                ins.then_inc(fc_g_ok, 1)
                dve.wait_ge(fc_mean_mm, 1)
                for c in range(IC):
                    ins = v.tensor_tensor(fc_c[:, c, :], fc_g[:, c, :], bank(3, D), ALU.subtract)
                ins.then_inc(fc_c_ok, 1)
                for m, n in ((2, 0), (5, 1)):
                    gate_m, sign = mod[:, m, :], gate_sign[:, n, :]
                    chain(v.tensor_scalar(sign, gate_m, -1.0, None, ALU.mult))
                    chain(v.tensor_tensor(gate_bias[:, n, :], sign, gate_m, ALU.max))
                    chain(v.tensor_scalar(sign, gate_m, 0.0, 2.0, ALU.is_ge, ALU.mult))
                    chain(v.tensor_scalar(sign, sign, -1.0, None, ALU.add))
                    chain(v.scalar_tensor_tensor(out=gate_m, in0=gate_bias[:, n, :], scalar=0.25, in1=sign,
                                                 op0=ALU.max, op1=ALU.mult))
                dve.wait_ge(bias_mm, 1)
                chain(v.tensor_tensor(z_bias[:, 0:1], ps[:, 3, 0:1], vec("fc_b"), ALU.add))
                v.tensor_scalar(z_bias[:, 1:2], z_bias[:, 0:1], 0.5, None, ALU.mult)
                v.tensor_copy(bias_o[:, 0:1], ps[:, 3, 1:2])
                v.tensor_copy(key_b[:, :], ps[:, 3, 2:4])
                v.tensor_tensor(bias_o[:, 1:2], ps[:, 3, 4:5], vec("d_bo"), ALU.add)
                chain(v.tensor_tensor(bias_o[:, 2:3], ps[:, 3, 5:6], vec("c_bo"), ALU.add))
                v.tensor_scalar(slot_o[:, :], part("slot_t"), bias_o[:, 1:2], None, ALU.add)
                v.tensor_scalar(gate_bias[:, 0, :], mod[:, 2, :], bias_o[:, 0:1], None, ALU.mult)
                v.tensor_scalar(gate_bias[:, 1, :], mod[:, 5, :], bias_o[:, 2:3], None,
                                ALU.mult).then_inc(setup_done_dve, 1)

            def stats(st, mv, srcs, st_ok, mv_ok, b):
                moments(st, srcs, st_ok)
                aggregate(st, mv, st_ok, mv_ok, b)

            def moments(st, srcs, st_ok):
                for i in range(TT):
                    ins = v.bn_stats(st[:, i, :], srcs[i])
                ins.then_inc(st_ok, 1)

            def aggregate(st, mv, st_ok, mv_ok, b):
                wait_alone(dve, st_ok, b + 1, dve_passed)
                for i in range(TT):
                    ins = v.bn_aggr(mv[:, i, :], st[:, i, :])
                ins.then_inc(mv_ok, 1)

            def x_tile(b, i):
                return x_in[:, bass.ds(b, 1), i, :].rearrange("p a d -> p (a d)")

            def convolved(c):
                return v.scalar_tensor_tensor(out=h[:, c, :], in0=conv_ps[c], scalar=conv_bh[:, c:c + 1],
                                              in1=g_silu2[:, c, :], op0=ALU.add, op1=ALU.mult)

            def slot(t):
                if exists(t + 1):
                    wait(dve, ev["hn_ok"], t + 2)
                    v.tensor_copy(hn_p[0][:, K - 1:K - 1 + T], hn_t[:, :]).then_inc(ev["hnhigh_ok"], 1)
                    wait(dve, ev["hnhigh_ok"], t + 2)
                    v.tensor_tensor(hn_p[1][:, K - 1:K - 1 + T], hn_t[:, :], hn_p[0][:, K - 1:K - 1 + T].bitcast(F32),
                                    ALU.subtract).then_inc(ev["hnlow_ok"], 1)
                if exists(t):
                    wait(dve, ev["hT_mm"], t + 1)
                    moments(sth, [hT_ps[:, i, :] for i in range(TT)], ev["sth_ok"])
                if exists(t):
                    aggregate(sth, mvh, ev["sth_ok"], ev["mvh_ok"], t)
                if exists(t - 1):
                    wait(dve, ev["rs2_ok"], t)
                    for i in range(TT):
                        ins = v.tensor_scalar(n2[:, i, :], x1_ps[:, i, :], mv2[:, i, 0:1], rs2[:, i:i + 1],
                                              ALU.subtract, ALU.mult)
                    ins.then_inc(ev["n2_ok"], 1)
                if exists(t - 2):
                    wait(dve, ev["av_mm"], t - 1)
                    v.tensor_tensor(att_m[:, :, :], av_ps, mask_r.unsqueeze(2).broadcast_to([P, HPC, S]),
                                    ALU.mult).then_inc(ev["attm_ok"], 1)
                    wait(dve, ev["attm_ok"], t - 1)
                    v.tensor_reduce(att_t[:, bass.ds(t - 2, 1), :].rearrange("p a s -> p (a s)"),
                                    att_m[:, :, :].rearrange("p h s -> p s h"), AX_X, ALU.add).then_inc(ev["at_ok"], 1)
                if exists(t + 2):
                    stats(st1, mv1, [x_tile(t + 2, i) for i in range(TT)], ev["st1_ok"], ev["mv1_ok"], t + 2)
                if exists(t + 1):
                    wait(dve, ev["gtanh_ok"], t + 2)
                    v.scalar_tensor_tensor(out=g_silu2[:, :, :], in0=g_tanh[:, :, :], scalar=1.0, in1=gate_ps,
                                           op0=ALU.add, op1=ALU.mult).then_inc(ev["gsilu_ok"], 1)
                if exists(t):
                    wait(dve, ev["ztanh_ok"], t + 1)
                    v.scalar_tensor_tensor(out=z_silu2[:, :], in0=z_tanh[:, :], scalar=1.0, in1=z[:, :],
                                           op0=ALU.add, op1=ALU.mult).then_inc(ev["zsilu_ok"], 1)
                if exists(t - 1):
                    wait(dve, ev["s_mm"], t)
                    v.tensor_reduce(mx[:, :], s_ps, AX_X, ALU.max).then_inc(ev["mx_ok"], 1)
                    wait(dve, ev["mx_ok"], t)
                    v.tensor_tensor(mxb[:, :], mx[:, :], key_b[:, :], ALU.add).then_inc(ev["mxb_ok"], 1)
                    wait(dve, ev["mxb_ok"], t)
                    v.tensor_tensor(ebias[:, :], key_b[:, :], mxb[:, :], ALU.subtract).then_inc(ev["ebias_ok"], 1)
                if exists(t + 2):
                    wait(dve, ev["rs1_ok"], t + 3)
                    wait(dve, ev["hn_mm"], t + 2)
                    for i in range(TT):
                        ins = v.tensor_scalar(n1[:, i, :], x_tile(t + 2, i), mv1[:, i, 0:1], rs1[:, i:i + 1],
                                              ALU.subtract, ALU.mult)
                    ins.then_inc(ev["n1_ok"], 1)
                if exists(t + 1):
                    wait(dve, ev["gsilu_ok"], t + 2)
                    wait(dve, ev["conv0_mm"], t + 2)
                    wait(dve, ev["h0_used"], t + 1)
                    convolved(0)
                if exists(t - 1):
                    wait(dve, ev["exp_ok"], t)
                    v.reciprocal(rsum[:, :], psum[:, :]).then_inc(ev["rsum_ok"], 1)
                    wait(dve, ev["rsum_ok"], t)
                    for c in range(HC):
                        ins = v.tensor_scalar(prob[:, c, :], prob[:, c, :], rsum[:, c:c + 1], None, ALU.mult)
                    ins.then_inc(ev["prob_ok"], 1)
                if exists(t):
                    wait(dve, ev["xb_ok"], t + 1)
                    wait(dve, ev["x1_kept"], t)
                    wait(dve, ev["out_mm"], t + 1)
                    v.scalar_tensor_tensor(out=x1[:, :], in0=out_ps, scalar=mod[:, 2, bass.ds(t, 1)],
                                           in1=xres[:, bass.ds(t, 1), :].rearrange("p a t -> p (a t)"),
                                           op0=ALU.mult, op1=ALU.add).then_inc(ev["x1_ok"], 1)
                if exists(t + 1):
                    wait(dve, ev["conv_mm"], t + 2)
                    convolved(1).then_inc(ev["h_ok"], 1)
                if exists(t):
                    wait(dve, ev["x1_mm"], t + 1)
                    stats(st2, mv2, [x1_ps[:, i, :] for i in range(TT)], ev["st2_ok"], ev["mv2_ok"], t)

            dve.wait_ge(x_in_sem[0], 16)
            slot(FIRST)
            setup_of_first_slots()
            slot(FIRST + 1)
            setup_of_later_steps()
            dve.wait_ge(x_in_sem[1], 16)
            for t in range(FIRST + 2, LOOP[0]):
                slot(t)
            for s_ in x_in_sem[2:]:
                dve.wait_ge(s_, 16)
            with dve.Fori(*LOOP) as t:
                slot(t)
            for t in range(LOOP[1], LAST + 1):
                slot(t)

            dve.wait_ge(late_in, 16)
            dve.wait_ge(o_mm, 1)
            v.tensor_tensor(o_t[:, :, :], bank(0, NS, S), over_samples(slot_o[:, :]), ALU.add).then_inc(o_ok, 1)
            dve.wait_ge(oT_mm, 1)
            for i in range(2):
                ins = v.bn_stats(st3[:, i, :], ps[:, 1, i * P:(i + 1) * P])
            ins.then_inc(e_chain, 1)
            dve.wait_ge(e_chain, 1)
            for i in range(2):
                ins = v.bn_aggr(mv3[:, i, :], st3[:, i, :])
            ins.then_inc(e_chain, 1)
            dve.wait_ge(e_pool, 2)
            for i in range(2):
                ins = v.tensor_scalar(n3[:, i, :], ps[:, 1, i * P:(i + 1) * P], mv3[:, i, 0:1], rs3[:, i:i + 1],
                                      ALU.subtract, ALU.mult)
            ins.then_inc(e_chain, 1)
            v.tensor_tensor(o_t[:, :, :], o_t[:, :, :], over_samples(late("e_b2_t")), ALU.add)
            dve.wait_ge(eT_mm, 1)
            chain(v.tensor_tensor(ng3[:, :, :], bank(2, NS, S), over_samples(late("e_g_t")), ALU.mult))
            v.tensor_tensor(he_t[:, :, 0:NS].rearrange("p s b -> p b s"), ng3[:, :, :], over_samples(late("e_b_t")),
                            ALU.add).then_inc(he_ok, 1)
            dve.wait_ge(expert_in, EXPERT_LOADS)

            def hidden_biases(g):
                for n, (b, dst) in enumerate(((b1, ub), (bg, gb_))):
                    dve.wait_ge(u_mm, 2 * g + n + 1)
                    if g >= 2:
                        dve.wait_ge(us_ok, g - 1)
                    v.tensor_tensor(dst[:, g % 2, :], ps[:, 4 + 2 * n + g % 2, :], b[:, g, :],
                                    ALU.add).then_inc(ub_ok, 1)

            def gated(g):
                dve.wait_ge(us_ok, g + 1)
                if g >= 2:
                    dve.wait_ge(ugT_mm, g - 1)
                v.tensor_tensor(ug[:, g % 2, :], us[:, g % 2, :], gs[:, g % 2, :], ALU.mult).then_inc(ug_ok, 1)

            def add_to_slots(g):
                dve.wait_ge(yeT_mm, g + 1)
                e = slice(EG * g, EG * (g + 1))
                y = ps[:, g % 2, 0:P].rearrange("p (j q) -> p q j", j=EG)[:, 0:NS, :]
                v.tensor_tensor(o2_t[:, :, e], o_t[:, :, e], y, ALU.add).then_inc(o2_ok, 1)

            for g in range(NG + 3):
                if g < NG:
                    hidden_biases(g)
                if 1 <= g < NG + 1:
                    gated(g - 1)
                if g >= 3:
                    add_to_slots(g - 3)
            dve.wait_ge(k2_mm, 1)
            v.tensor_scalar(k2_t[:, :, :], bank(4, NS, S), vec("c_bk"), None, ALU.add).then_inc(k2_ok, 1)

            dve.wait_ge(v2_mm, 1)
            v.tensor_copy(v2_t[:, :, :], bank(5, NS, S)).then_inc(v2_ok, 1)

            def slot2(t, parity):
                if exists(t - 1):
                    for i, half in enumerate(("e2_half", "e2_ok")):
                        wait(dve, f[half], t)
                        ins = v.tensor_reduce(sum2[:, i, :], by_head(e2_of[1 - parity][:, i, :]), AX_X, ALU.add)
                    ins.then_inc(f["sum2_ok"], 1)
                if exists(t):
                    wait(dve, f["s2_mm"], t + 1)
                    v.tensor_reduce(mx2[:, :, :], s2_ps_of[parity].rearrange("p i (h s) -> p (i h) s", s=S), AX_X,
                                    ALU.max).then_inc(f["mx2_ok"], 1)
                if exists(t - 1):
                    wait(dve, f["sum2_ok"], t)
                    wait(dve, f["p2_ok"], t - 1)
                    v.reciprocal(rsum2[:, :, :], sum2[:, :, :]).then_inc(f["rsum2_ok"], 1)
                if exists(t):
                    wait(dve, f["mx2_ok"], t + 1)
                    for i, half in enumerate(("s2_half", "s2_ok")):
                        v.tensor_tensor(by_head(s2_rows[:, i, :]), by_head(s2_ps_of[parity][:, i, :]),
                                        mx2[:, i, :].unsqueeze(2).broadcast_to([P, H, S]),
                                        ALU.subtract).then_inc(f[half], 1)
                if exists(t - 1):
                    wait(dve, f["p2T_mm"], t - 1)
                    wait(dve, f["rsum2_ok"], t)
                    v.tensor_tensor(by_head(p2[:, 0, :]), by_head(e2_of[1 - parity][:, 0, :]),
                                    rsum2[:, 0, :].unsqueeze(2).broadcast_to([P, H, S]),
                                    ALU.mult).then_inc(f["p2_half"], 1)

            for t in range(0, LOOP2[0]):
                slot2(t, t % 2)
            with dve.Fori(*LOOP2) as t:
                slot2(t, LOOP2[0] % 2)
                slot2(t + 1, (LOOP2[0] + 1) % 2)
            for t in range(LOOP2[1], LAST2 + 1):
                slot2(t, t % 2)


def kernel(**inputs):
    import concourse.bacc as bacc
    from concourse.bass_utils import run_bass_kernel_spmd

    a = {k: np.asarray(v) for k, v in inputs.items()}

    def attn(name):
        return a["L0_attn_" + name]

    def ffn(name):
        return a["L0_ffn_" + name]

    def by_rows(w):
        return w.reshape(-1, P, w.shape[-1]).transpose(1, 0, 2).reshape(P, -1)

    feature = np.arange(D)
    mask_j = (feature[:, None] // DH == np.arange(H)).astype(np.float32)
    mask_r = (feature[:, None] % JC // DH == np.arange(HPC)).astype(np.float32)

    x = attn("hidden_states")
    w_in = attn("in_proj_w")
    vecs = {
        "conv_b": attn("conv_b"), "ln_g": attn("ln_g"), "ln_b": attn("ln_b"), "cproj_b": attn("cproj_b"),
        "fc_b": attn("fc_b"), "d_bq": ffn("d_bq"), "d_bk": ffn("d_bk"), "d_bv": ffn("d_bv"), "d_bo": ffn("d_bo"),
        "c_bq": ffn("c_bq"), "c_bk": ffn("c_bk"), "c_bv": ffn("c_bv"), "c_bo": ffn("c_bo")}
    vec = np.stack([vecs[n] if n in vecs else vecs[n[:-1]][int(n[-1]) * P:(int(n[-1]) + 1) * P] for n in VEC], 1)
    setup = {
        "ident": np.eye(P, dtype=np.float32), "c_t": a["L0_c"].T, "slot_t": ffn("slot_query")[0].T, "vec": vec,
        "pad": np.zeros((P, 3), np.float32), "wmod": a["L0_wmod"], "w_h": by_rows(w_in[:I]), "w_gate_t": w_in[I:].T,
        "fc_t": by_rows(attn("fc_w").T), "out_t": by_rows(attn("out_w").T), "cproj": by_rows(attn("cproj_w")),
        "conv_w": attn("conv_w").reshape(IC, G // IC, CG, CG, K).transpose(1, 3, 0, 4, 2).reshape(P, -1),
        "d_wq": ffn("d_Wq"), "d_wk_t": ffn("d_Wk").T, "d_wv": ffn("d_Wv"), "d_wo": ffn("d_Wo"),
        "c_wq": ffn("c_Wq"), "c_wo": ffn("c_Wo"), "mask_j": mask_j, "mask_r": mask_r}
    late = {
        "c_wk": ffn("c_Wk"), "c_wv": ffn("c_Wv"), "e_g_t": ffn("e_ln_g").T, "e_b_t": ffn("e_ln_b").T,
        "e_b2_t": ffn("e_b2").T}
    arrays = {
        "x_tok": x.reshape(NS, TT, P, D).transpose(2, 0, 1, 3),
        "x_feat": x.transpose(2, 0, 1),
        "setup_w": np.concatenate([setup[n] for n in SETUP_PARTS], 1),
        "late_w": np.concatenate([late[n] for n in LATE_PARTS], 1),
        "e_w1": ffn("e_W1").transpose(1, 0, 2),
        "e_wg": ffn("e_Wg").transpose(1, 0, 2),
        "e_w2": ffn("e_W2").reshape(S, FC, P, D).transpose(2, 0, 1, 3),
        "e_b1": ffn("e_b1"),
        "e_bg": ffn("e_bg"),
    }
    arrays = {k: np.ascontiguousarray(v) for k, v in arrays.items()}
    nc = bacc.Bacc("TRN2", target_bir_lowering=False, num_devices=1)
    args = {k: nc.dram_tensor(k, v.shape, F32, kind="ExternalInput").ap() for k, v in arrays.items()}
    out = nc.dram_tensor("out", (P, NS, T), F32, kind="ExternalOutput").ap()
    adaln_block_kernel(nc, **args, out=out)
    r = run_bass_kernel_spmd(nc, [arrays], core_ids=[0])
    return np.ascontiguousarray(r.results[0]["out"].transpose(1, 2, 0))
```
